# Optimizing a Trainium2 kernel written in Bass

```python
import numpy as np
import jax
import jax.numpy as jnp

def _softmax(x, axis=-1):
    return jax.nn.softmax(x, axis=axis)

def _gelu(x):
    return jax.nn.gelu(x, approximate=True)

def _silu(x):
    return jax.nn.silu(x)

def _sigmoid(x):
    return jax.nn.sigmoid(x)

def _layernorm(x, axis=-1, eps=1e-05):
    m = jnp.mean(x, axis=axis, keepdims=True)
    v = jnp.var(x, axis=axis, keepdims=True)
    return (x - m) / jnp.sqrt(v + eps)

def _scatter_add(tgt, idx, src, axis=0):
    return tgt.at[idx].add(src)

def _segment_sum(src, seg, n):
    return jax.ops.segment_sum(src, seg, n)
kernel_name = 'mk_seq_postln_d1_jaxref_r8_7f1e28'

def setup_inputs(seed: int=0):
    np.random.seed(seed)
    _w = jnp.asarray

    def _L0_attn_setup():
        import jax, jax.numpy as jnp
        import numpy as np
        HIDDEN = 256
        N_HEADS = 16
        HEAD_DIM = HIDDEN // N_HEADS

        def rotate_half(x):
            x1, x2 = jnp.split(x, 2, axis=-1)
            return jnp.concatenate([-x2, x1], axis=-1)
        key = jax.random.key(seed)
        k0, k1, k2, k3, k4 = jax.random.split(key, 5)
        B, S = (1, 256)
        scale = 1.0 / np.sqrt(HIDDEN)
        return {'hidden_states': jax.random.normal(k0, (B, S, HIDDEN), dtype=jnp.float32), 'Wq': jax.random.normal(k1, (HIDDEN, HIDDEN), dtype=jnp.float32) * scale, 'Wk': jax.random.normal(k2, (HIDDEN, HIDDEN), dtype=jnp.float32) * scale, 'Wv': jax.random.normal(k3, (HIDDEN, HIDDEN), dtype=jnp.float32) * scale, 'Wo': jax.random.normal(k4, (HIDDEN, HIDDEN), dtype=jnp.float32) * scale, 'gate': jnp.zeros((1, N_HEADS, 1, 1), dtype=jnp.float32)}
    _L0_attn_in = _L0_attn_setup()

    def _L0_ffn_setup():
        import jax, jax.numpy as jnp
        import numpy as np
        B, S, H = (2, 128, 256)
        E, K, F = (8, 2, 176)
        N_SHARED = 2
        FS = F * N_SHARED
        ROUTED_SCALE = 1.0

        def _swiglu_mlp(x, wg, wu, wd):
            return jax.nn.silu(x @ wg.T) * (x @ wu.T) @ wd.T
        key = jax.random.key(seed)
        ks = jax.random.split(key, 8)

        def w(k, shape, fan_in):
            return jax.random.normal(k, shape, jnp.float32) * (1.0 / np.sqrt(fan_in))
        return {'hidden_states': jax.random.normal(ks[0], (B, S, H), jnp.float32), 'gate_weight': w(ks[1], (E, H), H), 'w_gate': w(ks[2], (E, F, H), H), 'w_up': w(ks[3], (E, F, H), H), 'w_down': w(ks[4], (E, H, F), F), 'sw_gate': w(ks[5], (FS, H), H), 'sw_up': w(ks[6], (FS, H), H), 'sw_down': w(ks[7], (H, FS), FS)}
    _L0_ffn_in = _L0_ffn_setup()
    _d = {'L0_attn_hidden_states': _L0_attn_in['hidden_states'], 'L0_attn_Wq': _L0_attn_in['Wq'], 'L0_attn_Wk': _L0_attn_in['Wk'], 'L0_attn_Wv': _L0_attn_in['Wv'], 'L0_attn_Wo': _L0_attn_in['Wo'], 'L0_attn_gate': _L0_attn_in['gate'], 'L0_ffn_gate_weight': _L0_ffn_in['gate_weight'], 'L0_ffn_w_gate': _L0_ffn_in['w_gate'], 'L0_ffn_w_up': _L0_ffn_in['w_up'], 'L0_ffn_w_down': _L0_ffn_in['w_down'], 'L0_ffn_sw_gate': _L0_ffn_in['sw_gate'], 'L0_ffn_sw_up': _L0_ffn_in['sw_up'], 'L0_ffn_sw_down': _L0_ffn_in['sw_down']}
    _x0 = _d['L0_attn_hidden_states']
    _d['L0_attn_hidden_states'] = jax.random.normal(jax.random.fold_in(jax.random.key(seed), 1), (4, 512, 256), dtype=_x0.dtype)
    del _x0
    return _d

def reference(L0_attn_hidden_states, L0_attn_Wq, L0_attn_Wk, L0_attn_Wv, L0_attn_Wo, L0_attn_gate, L0_ffn_gate_weight, L0_ffn_w_gate, L0_ffn_w_up, L0_ffn_w_down, L0_ffn_sw_gate, L0_ffn_sw_up, L0_ffn_sw_down):

    def _L0_attn_ref(hidden_states, Wq, Wk, Wv, Wo, gate):
        import jax, jax.numpy as jnp
        import numpy as np
        HIDDEN = 256
        N_HEADS = 16
        HEAD_DIM = HIDDEN // N_HEADS

        def rotate_half(x):
            x1, x2 = jnp.split(x, 2, axis=-1)
            return jnp.concatenate([-x2, x1], axis=-1)
        B, S, H = hidden_states.shape
        q = hidden_states @ Wq.T
        k = hidden_states @ Wk.T
        v = hidden_states @ Wv.T
        inv_freq = 1.0 / 10000.0 ** (jnp.arange(0, H, 2, dtype=jnp.float32) / H)
        t = jnp.arange(S, dtype=jnp.float32)
        freqs = t[:, None] * inv_freq[None, :]
        emb = jnp.concatenate([freqs, freqs], axis=-1)[None]
        cos, sin = (jnp.cos(emb), jnp.sin(emb))
        q = q * cos + rotate_half(q) * sin
        k = k * cos + rotate_half(k) * sin

        def split_heads(x):
            return x.reshape(B, S, N_HEADS, HEAD_DIM).transpose(0, 2, 1, 3)
        q, k, v = (split_heads(q), split_heads(k), split_heads(v))
        k_feat = jax.nn.elu(k) + 1.0
        memory = jnp.einsum('bhsd,bhse->bhde', k_feat, v)
        norm_term = k_feat.sum(axis=2)
        q_feat = jax.nn.elu(q) + 1.0
        mem_out = jnp.einsum('bhsd,bhde->bhse', q_feat, memory)
        denom = jnp.einsum('bhsd,bhd->bhs', q_feat, norm_term)[..., None]
        mem_out = mem_out / denom
        scale = 1.0 / jnp.sqrt(jnp.float32(HEAD_DIM))
        scores = jnp.einsum('bhqd,bhkd->bhqk', q, k) * scale
        attn = jnp.einsum('bhqk,bhkd->bhqd', jax.nn.softmax(scores, axis=-1), v)
        g = jax.nn.sigmoid(gate)
        combined = g * mem_out + (1.0 - g) * attn
        combined = combined.transpose(0, 2, 1, 3).reshape(B, S, H)
        return combined @ Wo.T

    def _L0_ffn_ref(hidden_states, gate_weight, w_gate, w_up, w_down, sw_gate, sw_up, sw_down):
        import jax, jax.numpy as jnp
        import numpy as np
        B, S, H = (2, 128, 256)
        E, K, F = (8, 2, 176)
        N_SHARED = 2
        FS = F * N_SHARED
        ROUTED_SCALE = 1.0

        def _swiglu_mlp(x, wg, wu, wd):
            return jax.nn.silu(x @ wg.T) * (x @ wu.T) @ wd.T
        b, s, h = hidden_states.shape
        x = hidden_states.reshape(-1, h)
        T = x.shape[0]
        logits = x.astype(jnp.float32) @ gate_weight.astype(jnp.float32).T
        scores = jax.nn.softmax(logits, axis=-1)
        topk_w, topk_idx = jax.lax.top_k(scores, K)
        topk_w = topk_w / (jnp.sum(topk_w, axis=-1, keepdims=True) + 1e-20)
        topk_w = topk_w * ROUTED_SCALE
        cw = jnp.zeros((T, E), jnp.float32).at[jnp.arange(T)[:, None], topk_idx].add(topk_w)
        g = jax.nn.silu(jnp.einsum('th,efh->tef', x, w_gate)) * jnp.einsum('th,efh->tef', x, w_up)
        expert_out = jnp.einsum('tef,ehf->teh', g, w_down)
        y = jnp.einsum('te,teh->th', cw, expert_out).reshape(b, s, h)
        y = y + _swiglu_mlp(x, sw_gate, sw_up, sw_down).reshape(b, s, h)
        return y
    x = L0_attn_hidden_states
    x = _layernorm(x + _L0_attn_ref(x, L0_attn_Wq, L0_attn_Wk, L0_attn_Wv, L0_attn_Wo, L0_attn_gate), axis=-1)
    x = _layernorm(x + _L0_ffn_ref(x, L0_ffn_gate_weight, L0_ffn_w_gate, L0_ffn_w_up, L0_ffn_w_down, L0_ffn_sw_gate, L0_ffn_sw_up, L0_ffn_sw_down), axis=-1)
    return x

_drawn_inputs = setup_inputs


def setup_inputs(seed=0):
    import zlib

    import numpy as np

    out = dict(_drawn_inputs(seed))
    spreads = {'L0_attn_gate': (0.0, 0.742)}
    factors = {}
    for name, (base, spread) in spreads.items():
        noise = np.random.default_rng([zlib.crc32(name.encode()), seed]).standard_normal(out[name].shape)
        drawn = base * np.exp(spread * noise) if base else spread * noise
        out[name] = jnp.asarray(drawn.astype(out[name].dtype))
    for name, factor in factors.items():
        out[name] = (out[name] * factor).astype(out[name].dtype)
    return out
```

```python
from contextlib import ExitStack

import concourse.bass as bass
from concourse import mybir

F32 = mybir.dt.float32
BF16 = mybir.dt.bfloat16
ALU = mybir.AluOpType
ACT = mybir.ActivationFunctionType
AX_X = mybir.AxisListType.X

P = 128
B, S, H = 4, 512, 256
HEADS, D = 16, 16
TILES = S // P
HC = H // P
HG = 4
GB = HEADS // HG
NG = B * GB
UNITS = HG * TILES
SCALE = D ** -0.5
EPS = 1e-5
E, F, FS = 8, 176, 352
FALL = E * F + FS
NF = -(-FALL // P)
NFR = E * F // P
Q_PARTS = (0, 0, 1, 0, 2, 1)
K_PARTS = (0, 1, 0, 2, 0, 1)
KS = len(Q_PARTS) * D
RING = 6
LAG = 2
STACK_INC = 16 * 2 * len(Q_PARTS)
HRING = 17
FORDER = list(range(NFR, NF)) + list(range(NFR))


def frows(f):
    return min(P, FALL - f * P)


def stages(i, u):
    out = []
    for b in range(B):
        s = -3 + 4 * b
        plan = {
            (s, 0): ["q0"], (s, 2): ["q1", "rotate_q"], (s, 5): ["split1_q"], (s, 8): ["k0", "split2_q"],
            (s, 10): ["k1", "rotate_k"], (s, 11): ["expneg_q"], (s, 12): ["feat_q"],
            (s, 14): ["split1_k"],
            (s + 1, 2): ["split2_k"], (s + 1, 4): ["expneg_k"], (s + 1, 5): ["v0"],
            (s + 1, 6): ["feat_k"], (s + 1, 7): ["v1"],
            (s + 1, 13): ["kt0"], (s + 1, 15): ["kt1"],
            (s + 2, 13): ["memory"],
            (s + 3, 5): ["mem0"], (s + 3, 7): ["mem1"], (s + 3, 13): ["mem2"], (s + 3, 15): ["mem3"],
            (s + 9, 9): ["ct0"], (s + 9, 11): ["ct1"], (s + 9, 13): ["wo0"], (s + 9, 15): ["wo1"],
            (s + 10, 2): ["ln_sqrt"], (s + 10, 5): ["ln_apply"],
            (s + 10, 10): ["xt0"], (s + 10, 12): ["xt1"],
        }
        if i >= 0:
            out += [(n, b) for n in plan.get((i, u), ())]
        elif u == 0:
            for key in sorted(k for k in plan if k[0] < 0):
                out += [(n, b) for n in plan[key]] if b == 0 else []
    if u == 2 and 0 <= i - 1 < NG:
        out.append(("maxt", i - 1))
    if u == 4 and 0 <= i - LAG - 1 < NG:
        out.append(("o_out", i - LAG - 1))
    if u == 6 and 0 <= i - LAG - 1 < NG:
        out.append(("ot", i - LAG - 1))
    return out


BANKED = ("q0", "q1", "k0", "k1", "v0", "v1", "kt0", "kt1", "memory", "mem0", "mem1", "mem2", "mem3",
          "ct0", "ct1", "wo0", "wo1", "xt0", "xt1", "maxt", "ot")
ITERATIONS = range(-1, NG + LAG + 3)


def bank_turns():
    turn = {}
    for i in ITERATIONS:
        for u in range(UNITS):
            for s in stages(i, u):
                if s[0] in BANKED:
                    turn[s] = len(turn)
    return turn


def build_block(nc, x, xT, wqT, wkT, wvT, woT, gate, cos, sin, blockmask, ident, gwT, rank, select,
                wgT, wuT, wdT, out):
    TURN = bank_turns()
    GM = len(TURN)

    with ExitStack() as ctx:
        def sb(name, shape, dt=F32):
            return ctx.enter_context(nc.sbuf_tensor(name, shape, dt))

        def sem(name):
            return ctx.enter_context(nc.semaphore(name))

        banks = [ctx.enter_context(nc.psum_tensor(f"bank{n}", [P, 512], F32)) for n in range(8)]
        ps_score = banks[0:3]
        ps_max = banks[3:5]
        ps_o = banks[5]
        ps_gen = banks[6:8]
        ps_gate, ps_up, ps_cw, ps_y = banks[0:2], banks[2:4], banks[4:6], banks[6:8]

        xT_sb = sb("xT_sb", [P, HC, B * S])
        x_sb = sb("x_sb", [P, B * TILES, H])
        wq_sb, wk_sb, wv_sb, wo_sb = (sb(n, [P, HC, H]) for n in ("wq_sb", "wk_sb", "wv_sb", "wo_sb"))
        cs_sb = sb("cs_sb", [P, 2, S])
        mask_sb = sb("mask_sb", [P, 8, D + 1])
        ident_sb = sb("ident_sb", [P, P])
        gmix = sb("gmix", [P, 4, HEADS])
        eps_sb = sb("eps_sb", [P, 1])
        work = sb("work", [P, 7168])
        prod = work[:, 0:2048].rearrange("p (k t) -> p k t", k=4)
        rot = [work[:, 2048 + 1024 * t:3072 + 1024 * t].rearrange("p (c t) -> p c t", c=HC) for t in range(2)]
        part = [[work[:, 4096 + 512 * (3 * t + j):4608 + 512 * (3 * t + j)].bitcast(BF16)
                 .rearrange("p (c t) -> p c t", c=HC) for j in range(3)] for t in range(2)]
        wg_sb = work[:, 0:2 * FALL].rearrange("p (c f) -> p c f", c=HC)
        wu_sb = work[:, 2 * FALL:4 * FALL].rearrange("p (c f) -> p c f", c=HC)
        resid = sb("resid", [P, HC, S])
        neg = sb("neg", [P, HC, S])
        feat = [sb("feat_q", [P, HC, S]), sb("feat_k", [P, HC, S])]
        kf_tok = sb("kf_tok", [P, TILES, H])
        mem_bd = sb("mem_bd", [P, 2, HC, 8 * (D + 1)])
        mem_tok = sb("mem_tok", [P, 2, TILES, H])
        rden = sb("rden", [P, 2, HC, 8])
        stack = sb("stack", [P, RING * 2 * HG * S], BF16)
        qk = stack[:, :].rearrange("p (r w h t) -> p r w h t", r=RING, w=2, h=HG)
        hid = stack[:, 0:HRING * 2 * S].bitcast(F32).rearrange("p (n t) -> p n t", n=HRING)
        v_sb = sb("v_sb", [P, 2, TILES, HEADS, 2 * D])
        probs_w = sb("probs_w", [P, 8 * S])
        probs = probs_w[:, :].rearrange("p (n t) -> p n t", n=8)
        wd_sb = probs_w[:, 0:NF * H].rearrange("p (f n) -> p f n", f=NF)
        mx = sb("mx", [P, 2, UNITS])
        mneg = sb("mneg", [UNITS, 2, P])
        mres = sb("mres", [UNITS, P])
        mpart = [sb(f"mpart{j}", [UNITS, 2, P], BF16) for j in range(3)]
        o_sb = sb("o_sb", [P, 2, S])
        rsum = sb("rsum", [P, 2, TILES, HG])
        c_tok = sb("c_tok", [P, TILES, H])
        ct_sb = sb("ct_sb", [P, HC, S])
        stats = sb("stats", [P, TILES, 6])
        mv = sb("mv", [P, TILES, 2])
        std = sb("std", [P, 2, TILES])
        NT = B * TILES
        gw_sb = sb("gw_sb", [P, HC, E])
        rank_sb = sb("rank_sb", [P, E])
        rt = o_sb[:, 0, :].rearrange("p (k n e) -> p k n e", k=4, n=NT)
        rs = o_sb[:, 1, 0:8 * NT].rearrange("p (k n) -> p k n", k=8)
        cw3 = mem_tok[:, 0, 0:2, 0:192].rearrange("p a (n j) -> p a n j", j=3 * E)
        cwT = neg[0:3 * E, :, :].bitcast(BF16).rearrange("p c t -> p (c t)")
        sel_f = feat[0][0:3 * E, :, :].rearrange("p c t -> p (c t)")
        sel_f2 = feat[1][0:3 * E, :, :].rearrange("p c t -> p (c t)")
        sel_sb = resid[0:3 * E, :, :].bitcast(BF16).rearrange("p c t -> p (c t)")
        gact = [c_tok[:, 2 * n:2 * n + 2, :].rearrange("p a b -> p (a b)") for n in range(2)]
        hmid = [ct_sb[:, n, :] for n in range(2)]

        ld_qk = sem("ld_qk"); ld_x0 = sem("ld_x0"); ld_v = sem("ld_v"); ld_cs = sem("ld_cs"); ld_late = sem("ld_late")
        ld_gu = sem("ld_gu"); ld_down = sem("ld_down"); ld_sel = sem("ld_sel")
        ready = sem("ready")
        taken = sem("taken")
        max_ready = sem("max_ready"); max_taken = sem("max_taken")
        score_ready = sem("score_ready"); exp_done = sem("exp_done")
        pv_done = sem("pv_done"); o_taken = sem("o_taken")
        rotated = sem("rotated")
        split1 = sem("split1"); resid_ready = sem("resid_ready"); split2 = sem("split2"); split3 = sem("split3")
        neg_ready = sem("neg_ready"); expneg = sem("expneg"); feat_ready = sem("feat_ready")
        stacked = [sem(f"stacked{r}") for r in range(RING)]
        mneg_split = sem("mneg_split"); maxed = [sem(f"maxed{r}") for r in range(2)]
        sigm = sem("sigm"); init_v = sem("init_v"); init_p = sem("init_p")
        stats_ready = sem("stats_ready"); std_ready = sem("std_ready"); normed = sem("normed")
        vch = sem("vch"); pch = sem("pch")
        logits = sem("logits"); centred = sem("centred"); exped = sem("exped")
        cw_ready = sem("cw_ready"); cwT_ready = sem("cwT_ready")
        gate_ready = sem("gate_ready"); up_ready = sem("up_ready"); cwb_ready = sem("cwb_ready")
        silu_done = sem("silu_done"); hid_ready = sem("hid_ready"); up_taken = sem("up_taken")
        y_ready = sem("y_ready"); y_taken = sem("y_taken")
        stored = sem("stored")

        def slots():
            for i in ITERATIONS:
                for u in range(UNITS):
                    yield i, u

        def after_stack(eng, G):
            eng.wait_ge(stacked[G % RING], STACK_INC * (G // RING + 1))

        block = ctx.enter_context(nc.Block())

        @block.sync
        def _(sp):
            sp.dma_start(wq_sb[:], wqT.rearrange("(c p) n -> p c n", p=P)).then_inc(ld_qk, 16)
            sp.dma_start(xT_sb[:, :, 0:S], xT[:, 0:S].rearrange("(c p) t -> p c t", p=P)).then_inc(ld_x0, 16)
            sp.dma_start(cs_sb[:, 0, :], cos).then_inc(ld_cs, 16)
            sp.dma_start(cs_sb[:, 1, :], sin).then_inc(ld_cs, 16)
            sp.dma_start(wk_sb[:], wkT.rearrange("(c p) n -> p c n", p=P)).then_inc(ld_qk, 16)
            sp.dma_start(wv_sb[:], wvT.rearrange("(c p) n -> p c n", p=P)).then_inc(ld_v, 16)
            late = [(gmix[:, 0, :], gate.broadcast_to([P, HEADS])), (ident_sb[:], ident),
                    (mask_sb[:], blockmask.rearrange("p (h d) -> p h d", h=8)),
                    (xT_sb[:, :, S:], xT[:, S:].rearrange("(c p) t -> p c t", p=P)),
                    (wo_sb[:], woT.rearrange("(c p) n -> p c n", p=P)),
                    (x_sb[:], x.rearrange("(n p) h -> p n h", p=P)),
                    (gw_sb[:], gwT.rearrange("(c p) n -> p c n", p=P)),
                    (rank_sb[:], rank)]
            for dst, src in late:
                sp.dma_start(dst, src).then_inc(ld_late, 16)

            def stack_group(G):
                b, g = G // GB, G % GB
                if G >= RING:
                    sp.wait_ge(score_ready, UNITS * (G - RING + 1))
                r0 = 64 * (g % 2)
                for w, parts in ((0, Q_PARTS), (1, K_PARTS)):
                    sp.wait_ge(split3, 2 * b + w + 1)
                    for n, j in enumerate(parts):
                        sp.dma_start(qk[n * D:(n + 1) * D, G % RING, w, :, :],
                                     part[w][j][r0:r0 + 64, g // 2, :]).then_inc(stacked[G % RING], 16)

            for G in range(GB):
                stack_group(G)
            for i in range(1, NG + 1):
                G = i - 1
                sp.wait_ge(mneg_split, G + 1)
                for j in range(3):
                    sp.dma_start(qk[KS + j:KS + j + 1, G % RING, 0, :, :], mpart[j][:, G % 2, :])\
                        .then_inc(maxed[G % 2], 16)
                for G in range(GB, NG):
                    if i == max(GB * (G // GB) - 2, G - 3):
                        stack_group(G)
                if i == NG - 2:
                    for G in range(NG - GB, NG):
                        after_stack(sp, G)
                    sp.wait_ge(feat_ready, 2 * B)
                    sp.dma_start(wg_sb, wgT.rearrange("(c p) f -> p c f", p=P)).then_inc(ld_gu, 16)
                    sp.dma_start(wu_sb, wuT.rearrange("(c p) f -> p c f", p=P)).then_inc(ld_gu, 16)
                    sp.dma_start(sel_f, select[:, 0:1024]).then_inc(ld_sel, 16)
                    sp.wait_ge(ready, TURN[("kt1", B - 1)] + 1)
                    sp.dma_start(sel_f2[:, 0:NFR * P - 1024], select[:, 1024:NFR * P]).then_inc(ld_sel, 16)
            sp.wait_ge(pv_done, NG * TILES)
            sp.dma_start(wd_sb[:, 0:NF - 1, :], wdT[0:(NF - 1) * P, :].rearrange("(f p) n -> p f n", p=P)).then_inc(ld_down, 16)
            sp.dma_start(wd_sb[0:frows(NF - 1), NF - 1, :], wdT[(NF - 1) * P:FALL, :]).then_inc(ld_down, 16)
            for b in range(B):
                sp.wait_ge(normed, B + b + 1)
                sp.dma_start(out[b * S:(b + 1) * S, :].rearrange("(n p) h -> p n h", p=P),
                             x_sb[:, b * TILES:(b + 1) * TILES, :]).then_inc(stored, 16)
            sp.wait_ge(stored, 16 * B)

        @block.tensor
        def _(pe):
            def open_turn(s):
                n = TURN[s]
                if n >= 2:
                    pe.wait_ge(taken, n - 1)
                return ps_gen[n % 2]

            def project(dst, w, b, c):
                for k in range(HC):
                    ins = nc.tensor.matmul(dst[:, 0:S], w[:, k, c * P:(c + 1) * P],
                                           xT_sb[:, k, b * S:(b + 1) * S], start=(k == 0), stop=(k == HC - 1))
                return ins

            def banked(s):
                name, b = s
                g = open_turn(s)
                kind, n = name.rstrip("0123"), int(name[-1]) if name[-1].isdigit() else 0
                if kind == "q":
                    if b == 0 and n == 0:
                        pe.wait_ge(ld_qk, 32); pe.wait_ge(ld_x0, 16)
                    if b == 1 and n == 0:
                        pe.wait_ge(ld_late, 16 * 8)
                    ins = project(g, wq_sb, b, n)
                elif kind == "k":
                    ins = project(g, wk_sb, b, n)
                elif kind == "v":
                    if b == 0 and n == 0:
                        pe.wait_ge(ld_v, 16)
                    for t in range(2):
                        t0 = b * S + (2 * n + t) * P
                        for k in range(HC):
                            ins = nc.tensor.matmul(g[:, t * H:(t + 1) * H], xT_sb[:, k, t0:t0 + P], wv_sb[:, k, :],
                                                   start=(k == 0), stop=(k == HC - 1))
                elif kind == "kt":
                    if b == 0 and n == 0:
                        pe.wait_ge(ld_late, 16 * 8)
                    pe.wait_ge(feat_ready, 2 * b + 2)
                    for t in range(2):
                        for c in range(HC):
                            o = (t * HC + c) * P
                            t0 = (2 * n + t) * P
                            ins = nc.tensor.transpose(g[:, o:o + P], feat[1][:, c, t0:t0 + P], ident_sb[:])
                elif kind == "memory":
                    pe.wait_ge(taken, TURN[("kt1", b)] + 1)
                    for c in range(HC):
                        for t in range(TILES):
                            ins = nc.tensor.matmul(g[:, c * 136:c * 136 + 136], kf_tok[:, t, c * P:(c + 1) * P],
                                                   v_sb[:, b % 2, t, 8 * c:8 * c + 8, 0:D + 1],
                                                   start=(t == 0), stop=(t == TILES - 1))
                elif kind == "mem":
                    pe.wait_ge(taken, TURN[("memory", b)] + 1)
                    pe.wait_ge(feat_ready, 2 * b + 1)
                    for c in range(HC):
                        ins = nc.tensor.matmul(g[:, c * 136:c * 136 + 136], feat[0][:, c, n * P:(n + 1) * P],
                                               mem_bd[:, b % 2, c, :], start=True, stop=True)
                elif kind == "maxt":
                    pe.wait_ge(max_taken, UNITS * (b + 1))
                    ins = nc.tensor.transpose(g[0:UNITS, 0:P], mx[:, b % 2, :], ident_sb[:])
                elif kind == "ot":
                    pe.wait_ge(o_taken, b + 1)
                    for t in range(TILES):
                        ins = nc.tensor.transpose(g[:, t * P:(t + 1) * P], o_sb[:, b % 2, t * P:(t + 1) * P], ident_sb[:])
                elif kind == "ct":
                    pe.wait_ge(taken, TURN[("ot", GB * b + GB - 1)] + 1)
                    for c in range(HC):
                        for t in range(2):
                            o = (c * 2 + t) * P
                            ins = nc.tensor.transpose(g[:, o:o + P], c_tok[:, 2 * n + t, c * P:(c + 1) * P], ident_sb[:])
                elif kind == "wo":
                    pe.wait_ge(taken, TURN[(f"ct{n}", b)] + 1)
                    for t in range(2):
                        for c in range(HC):
                            ins = nc.tensor.matmul(g[:, t * H:(t + 1) * H], ct_sb[:, c, (2 * n + t) * P:(2 * n + t + 1) * P],
                                                   wo_sb[:, c, :], start=(c == 0), stop=(c == HC - 1))
                elif kind == "xt":
                    pe.wait_ge(normed, b + 1)
                    for c in range(HC):
                        for t in range(2):
                            o = (c * 2 + t) * P
                            ins = nc.tensor.transpose(g[:, o:o + P], x_sb[:, b * TILES + 2 * n + t, c * P:(c + 1) * P],
                                                      ident_sb[:])
                ins.then_inc(ready, 1)

            def value_product(m):
                G, t = m // TILES, m % TILES
                b = G // GB
                pe.wait_ge(exp_done, HG * (m + 1))
                if t == 0:
                    if G % GB == 0:
                        pe.wait_ge(taken, TURN[("v1", b)] + 1)
                    if G >= 1:
                        pe.wait_ge(o_taken, G)
                for h in range(HG):
                    ins = nc.tensor.matmul(ps_o[32 * h:32 * h + 32, :], v_sb[:, b % 2, t, (G % GB) * HG + h, :],
                                           probs[:, (HG * m + h) % 8, :], start=(t == 0), stop=(t == TILES - 1))
                ins.then_inc(pv_done, 1)

            for i, u in slots():
                t, h = u // HG, u % HG
                if 0 <= i < NG:
                    if u == 0:
                        after_stack(pe, i)
                    n = UNITS * i + u
                    if n >= 2:
                        pe.wait_ge(max_taken, n - 1)
                    nc.tensor.matmul(ps_max[n % 2][:, :], qk[0:KS, i % RING, 0, h, t * P:(t + 1) * P],
                                     qk[0:KS, i % RING, 1, h, :], start=True, stop=True).then_inc(max_ready, 1)
                j = i - LAG
                if 0 <= j < NG:
                    if u == 0:
                        pe.wait_ge(maxed[j % 2], 48 * (j // 2 + 1))
                        if j == 0:
                            pe.wait_ge(init_p, 1)
                    n = UNITS * j + u
                    if n >= 3:
                        pe.wait_ge(exp_done, n - 2)
                    nc.tensor.matmul(ps_score[n % 3][:, :], qk[0:KS + 3, j % RING, 1, h, t * P:(t + 1) * P],
                                     qk[0:KS + 3, j % RING, 0, h, :], start=True, stop=True).then_inc(score_ready, 1)
                m = (UNITS * j + u - 6) // HG
                if (UNITS * j + u - 6) % HG == 0 and 0 <= m < NG * TILES:
                    value_product(m)
                for s in stages(i, u):
                    if s[0] in BANKED:
                        banked(s)

            for n in range(NT):
                if n == 0:
                    pe.wait_ge(taken, GM)
                for c in range(HC):
                    ins = nc.tensor.matmul(ps_cw[0][:, n * E:(n + 1) * E], xT_sb[:, c, n * P:(n + 1) * P], gw_sb[:, c, :],
                                           start=(c == 0), stop=(c == HC - 1))
            ins.then_inc(logits, 1)

            def down(b):
                if b == 0:
                    pe.wait_ge(ld_down, 32)
                pe.wait_ge(up_taken, NF * (b + 1))
                pe.wait_ge(hid_ready, NFR * (b + 1))
                for t in range(TILES):
                    if t % 2 == 0 and b > 0:
                        pe.wait_ge(y_taken, 2 * (b - 1) + t // 2 + 1)
                    dst = ps_y[t // 2][:, (t % 2) * H:(t % 2 + 1) * H]
                    for k, f in enumerate(FORDER):
                        R = frows(f)
                        ins = nc.tensor.matmul(dst, hid[0:R, (NF * b + k) % HRING, t * P:(t + 1) * P], wd_sb[0:R, f, :],
                                               start=(k == 0), stop=(k == NF - 1))
                    if t % 2:
                        ins.then_inc(y_ready, 1)

            pe.wait_ge(ld_gu, 32)
            for b in range(B):
                for k, f in enumerate(FORDER):
                    n = NF * b + k
                    R = frows(f)
                    if n >= 2:
                        pe.wait_ge(silu_done, n - 1)
                    for dst, w, s in ((ps_gate[n % 2], wg_sb, gate_ready), (ps_up[n % 2], wu_sb, up_ready)):
                        if s is up_ready and n >= 2:
                            pe.wait_ge(up_taken, n - 1)
                        for c in range(HC):
                            ins = nc.tensor.matmul(dst[0:R, :], w[:, c, f * P:f * P + R], xT_sb[:, c, b * S:(b + 1) * S],
                                                   start=(c == 0), stop=(c == HC - 1))
                        ins.then_inc(s, 1)
                    if f < NFR:
                        if b == 0 and f == 0:
                            pe.wait_ge(cw_ready, 1)
                            for q in range(B):
                                if q >= 2:
                                    pe.wait_ge(cwT_ready, q - 1)
                                for t in range(TILES):
                                    m = q * TILES + t
                                    ins = nc.tensor.transpose(ps_y[q % 2][0:3 * E, t * P:(t + 1) * P],
                                                              cw3[:, m // 8, m % 8, :], ident_sb[:])
                                ins.then_inc(ready, 1)
                            pe.wait_ge(cwT_ready, B)
                        m = NFR * b + f
                        if m >= 2:
                            pe.wait_ge(hid_ready, m - 1)
                        nc.tensor.matmul(ps_cw[m % 2][:, :], sel_sb[:, f * P:(f + 1) * P], cwT[:, b * S:(b + 1) * S],
                                         start=True, stop=True).then_inc(cwb_ready, 1)
                    if k == 1 and b > 0:
                        down(b - 1)
            down(B - 1)

        @block.scalar
        def _(act):
            act.wait_ge(ld_late, 16 * 8)
            nc.scalar.activation(gmix[:, 1, :], gmix[:, 0, :], ACT.Exp, scale=-1.0).then_inc(sigm, 1)
            for i, u in slots():
                j = i - LAG
                if 0 <= j < NG:
                    n = UNITS * j + u
                    act.wait_ge(score_ready, n + 1)
                    if n >= 8:
                        act.wait_ge(pv_done, n // HG - 1)
                    nc.scalar.activation(probs[:, n % 8, :], ps_score[n % 3][:, :], ACT.Exp, scale=SCALE)\
                        .then_inc(exp_done, 1)
                for name, b in stages(i, u):
                    if name == "o_out":
                        act.wait_ge(pv_done, TILES * (b + 1))
                        if b >= 2:
                            act.wait_ge(ready, TURN[("ot", b - 2)] + 1)
                        nc.scalar.activation(o_sb[:, b % 2, :], ps_o[:, :], ACT.Copy).then_inc(o_taken, 1)
                        continue
                    if name == "ln_sqrt":
                        act.wait_ge(taken, TURN[("wo1", b)] + 1)
                        act.wait_ge(init_v, 1)
                        nc.scalar.activation(std[:, 0, :], mv[:, :, 1], ACT.Sqrt, bias=eps_sb[:, 0:1])\
                            .then_inc(std_ready, 1)
                        continue
                    kind, w = name[:-2], int(name[-1] == "k")
                    k = 2 * b + w
                    if kind == "split1":
                        act.wait_ge(rotated, k + 1)
                        if b > 0:
                            for G in range(GB * (b - 1), GB * b):
                                after_stack(act, G)
                        nc.scalar.activation(part[w][0], rot[w], ACT.Copy).then_inc(split1, 1)
                    if kind == "split2":
                        act.wait_ge(resid_ready, k + 1)
                        nc.scalar.activation(part[w][1], resid[:], ACT.Copy).then_inc(split2, 1)
                    if kind == "expneg":
                        act.wait_ge(neg_ready, k + 1)
                        nc.scalar.activation(neg[:], neg[:], ACT.Exp).then_inc(expneg, 1)

            act.wait_ge(centred, 1)
            nc.scalar.activation(rt[:, 1, :, :], rt[:, 0, :, :], ACT.Exp).then_inc(exped, 1)
            for b in range(B):
                for k, f in enumerate(FORDER):
                    n = NF * b + k
                    R = frows(f)
                    act.wait_ge(gate_ready, n + 1)
                    if n >= 2:
                        act.wait_ge(up_taken, n - 1)
                    elif n == 0:
                        act.wait_ge(ready, GM)
                    nc.scalar.activation(gact[n % 2][0:R, :], ps_gate[n % 2][0:R, :], ACT.Silu).then_inc(silu_done, 1)
                    if k == 6 and b > 0:
                        act.wait_ge(stats_ready, b)
                        nc.scalar.activation(std[:, 0, :], mv[:, :, 1], ACT.Sqrt, bias=eps_sb[:, 0:1])\
                            .then_inc(std_ready, 1)
            act.wait_ge(stats_ready, B)
            nc.scalar.activation(std[:, 0, :], mv[:, :, 1], ACT.Sqrt, bias=eps_sb[:, 0:1]).then_inc(std_ready, 1)

        @block.gpsimd
        def _(pool):
            nc.gpsimd.memset(stack[KS:KS + 3, :], 1.0).then_inc(init_p, 1)
            pool.wait_ge(init_p, 1)
            chain = [0]

            def link(ins):
                chain[0] += 1
                ins.then_inc(pch, 1)
                pool.wait_ge(pch, chain[0])

            def rotate(b, w):
                k = 2 * b + w
                pool.wait_ge(taken, TURN[("k1" if w else "q1", b)] + 1)
                if b > 0:
                    pool.wait_ge(feat_ready, k - 1)
                nc.gpsimd.tensor_tensor(rot[w][:, 0, :], prod[:, 0, :], prod[:, 2, :], ALU.subtract)
                nc.gpsimd.tensor_tensor(rot[w][:, 1, :], prod[:, 3, :], prod[:, 1, :], ALU.add).then_inc(rotated, 1)
                pool.wait_ge(rotated, k + 1)
                if k > 0:
                    pool.wait_ge(feat_ready, k)
                nc.gpsimd.tensor_scalar(neg[:], rot[w], 0.0, None, ALU.min).then_inc(neg_ready, 1)
                pool.wait_ge(split1, k + 1)
                if k > 0:
                    pool.wait_ge(split3, k)
                nc.gpsimd.tensor_tensor(resid[:], rot[w], part[w][0], ALU.subtract).then_inc(resid_ready, 1)
                pool.wait_ge(split2, k + 1)
                nc.gpsimd.tensor_tensor(part[w][2], resid[:], part[w][1], ALU.subtract).then_inc(split3, 1)

            for i, u in slots():
                for name, b in stages(i, u):
                    if name in ("rotate_q", "rotate_k"):
                        rotate(b, int(name[-1] == "k"))
                    if name == "maxt":
                        G = b
                        pool.wait_ge(taken, TURN[("maxt", G)] + 1)
                        if G >= 2:
                            pool.wait_ge(maxed[G % 2], 48 * (G // 2))
                        m, pt = mneg[:, G % 2, :], [x[:, G % 2, :] for x in mpart]
                        link(nc.gpsimd.tensor_copy(pt[0], m))
                        link(nc.gpsimd.tensor_tensor(mres[:], m, pt[0], ALU.subtract))
                        link(nc.gpsimd.tensor_copy(pt[1], mres[:]))
                        nc.gpsimd.tensor_tensor(pt[2], mres[:], pt[1], ALU.subtract).then_inc(mneg_split, 1)

        @block.vector
        def _(dve):
            chain = [0]

            def link(ins):
                chain[0] += 1
                ins.then_inc(vch, 1)
                dve.wait_ge(vch, chain[0])

            nc.vector.memset(v_sb[:], 1.0)
            link(nc.vector.memset(eps_sb[:], EPS))
            nc.vector.memset(std[:], 1.0).then_inc(init_v, 1)

            def banked(s):
                name, b = s
                g = ps_gen[TURN[s] % 2]
                kind, n = name.rstrip("0123"), int(name[-1]) if name[-1].isdigit() else 0
                dve.wait_ge(ready, TURN[s] + 1)
                if kind in ("q", "k"):
                    k = 2 * b + int(kind == "k")
                    if k == 0 and n == 0:
                        dve.wait_ge(ld_cs, 32)
                    if k > 0 and n == 0:
                        dve.wait_ge(rotated, k)
                    nc.vector.tensor_tensor(prod[:, 2 * n, :] if n == 0 else prod[:, 3, :], g[:, :], cs_sb[:, 0, :], ALU.mult)
                    ins = nc.vector.tensor_tensor(prod[:, 1, :] if n == 0 else prod[:, 2, :], g[:, :], cs_sb[:, 1, :], ALU.mult)
                elif kind == "v":
                    if b >= 2:
                        dve.wait_ge(pv_done, NG // B * TILES * (b - 1))
                    ins = nc.vector.tensor_copy(v_sb[:, b % 2, 2 * n:2 * n + 2, :, 0:D],
                                                g[:, :].rearrange("p (t h d) -> p t h d", t=2, h=HEADS))
                elif kind == "kt":
                    ins = nc.vector.tensor_copy(kf_tok[:, 2 * n:2 * n + 2, :], g[:, :].rearrange("p (t f) -> p t f", t=2))
                elif kind == "memory":
                    for c in range(HC):
                        ins = nc.vector.tensor_tensor(mem_bd[:, b % 2, c, :].rearrange("p (h d) -> p h d", h=8),
                                                      g[:, c * 136:c * 136 + 136].rearrange("p (h d) -> p h d", h=8),
                                                      mask_sb[:], ALU.mult)
                elif kind == "mem":
                    gv = g[:, 0:HC * 136].rearrange("p (c h d) -> p c h d", c=HC, h=8)
                    link(nc.vector.reciprocal(rden[:, 0, :, :], gv[:, :, :, D]))
                    link(nc.vector.tensor_tensor(rden[:, 1, :, :], rden[:, 0, :, :],
                                                 gmix[:, 2, :].rearrange("p (c h) -> p c h", c=HC), ALU.mult))
                    for c in range(HC):
                        ins = nc.vector.tensor_tensor(
                            mem_tok[:, b % 2, n, c * P:(c + 1) * P].rearrange("p (h d) -> p h d", h=8),
                            gv[:, c, :, 0:D], rden[:, 1, c, :].unsqueeze(2).broadcast_to([P, 8, D]), ALU.mult)
                elif kind == "maxt":
                    if b >= 2:
                        dve.wait_ge(mneg_split, b - 1)
                    ins = nc.vector.tensor_scalar(mneg[:, b % 2, :], g[0:UNITS, 0:P], -1.0, None, ALU.mult)
                elif kind == "ot":
                    G, bb = b, b // GB
                    gv = g[:, :].rearrange("p (t h d) -> p t h d", t=TILES, h=HG)
                    h0 = (G % GB) * HG
                    link(nc.vector.reciprocal(rsum[:, 0, :, :], gv[:, :, :, D]))
                    link(nc.vector.tensor_tensor(rsum[:, 1, :, :], rsum[:, 0, :, :],
                                                 gmix[:, 3, h0:h0 + HG].unsqueeze(1).broadcast_to([P, TILES, HG]), ALU.mult))
                    if G % GB == 0 and bb > 0:
                        dve.wait_ge(ready, TURN[("ct1", bb - 1)] + 1)
                    for t in range(TILES):
                        ins = nc.vector.tensor_tensor(
                            c_tok[:, t, h0 * D:(h0 + HG) * D].rearrange("p (h d) -> p h d", h=HG),
                            gv[:, t, :, 0:D], rsum[:, 1, t, :].unsqueeze(2).broadcast_to([P, HG, D]), ALU.mult)
                    link(ins)
                    cv = c_tok[:, :, h0 * D:(h0 + HG) * D]
                    ins = nc.vector.tensor_tensor(cv, cv, mem_tok[:, bb % 2, :, h0 * D:(h0 + HG) * D], ALU.add)
                elif kind == "ct":
                    ins = nc.vector.tensor_copy(ct_sb[:, :, 2 * n * P:(2 * n + 2) * P],
                                                g[:, :].rearrange("p (c t) -> p c t", c=HC))
                elif kind == "wo":
                    n0 = b * TILES + 2 * n
                    link(nc.vector.tensor_tensor(x_sb[:, n0:n0 + 2, :], g[:, :].rearrange("p (t h) -> p t h", t=2),
                                                 x_sb[:, n0:n0 + 2, :], ALU.add))
                    for t in range(2):
                        ins = nc.vector.bn_stats(stats[:, 2 * n + t, :], x_sb[:, n0 + t, :])
                    link(ins)
                    for t in range(2):
                        ins = nc.vector.bn_aggr(mv[:, 2 * n + t, :], stats[:, 2 * n + t, :])
                elif kind == "xt":
                    ins = nc.vector.tensor_copy(xT_sb[:, :, b * S + 2 * n * P:b * S + (2 * n + 2) * P],
                                                g[:, :].rearrange("p (c t) -> p c t", c=HC))
                ins.then_inc(taken, 1)

            def normalise(b, k):
                dve.wait_ge(std_ready, k + 1)
                link(nc.vector.reciprocal(std[:, 1, :], std[:, 0, :]))
                for t in range(TILES):
                    row = x_sb[:, b * TILES + t, :]
                    ins = nc.vector.tensor_scalar(row, row, mv[:, t, 0:1], std[:, 1, t:t + 1], ALU.subtract, ALU.mult)
                ins.then_inc(normed, 1)

            for i, u in slots():
                if 0 <= i < NG:
                    n = UNITS * i + u
                    t, h = u // HG, u % HG
                    dve.wait_ge(max_ready, n + 1)
                    if u == 0 and i >= 2:
                        dve.wait_ge(ready, TURN[("maxt", i - 2)] + 1)
                    nc.vector.tensor_reduce(mx[:, i % 2, h * TILES + t:h * TILES + t + 1], ps_max[n % 2][:, :], AX_X, ALU.max)\
                        .then_inc(max_taken, 1)
                for s in stages(i, u):
                    name, b = s
                    if name in BANKED:
                        if s == ("mem0", 0):
                            dve.wait_ge(sigm, 1)
                            link(nc.vector.tensor_scalar(gmix[:, 2, :], gmix[:, 1, :], 1.0, None, ALU.add))
                            link(nc.vector.reciprocal(gmix[:, 2, :], gmix[:, 2, :]))
                            link(nc.vector.tensor_scalar(gmix[:, 3, :], gmix[:, 2, :], -1.0, 1.0, ALU.mult, ALU.add))
                        banked(s)
                    if name in ("feat_q", "feat_k"):
                        w = int(name[-1] == "k")
                        dve.wait_ge(expneg, 2 * b + w + 1)
                        dve.wait_ge(rotated, 2 * b + w + 1)
                        if b > 0:
                            dve.wait_ge(ready, TURN[("kt1" if w else "mem3", b - 1)] + 1)
                        nc.vector.scalar_tensor_tensor(out=feat[w][:], in0=rot[w], scalar=0.0, in1=neg[:],
                                                       op0=ALU.max, op1=ALU.add).then_inc(feat_ready, 1)
                    if name == "ln_apply":
                        normalise(b, b)

            dve.wait_ge(logits, 1)
            lg = ps_cw[0][:, 0:NT * E].rearrange("p (n e) -> p n e", e=E)

            def across(a):
                return a.unsqueeze(2).broadcast_to([P, NT, E])

            link(nc.vector.tensor_reduce(rs[:, 0, :], lg, AX_X, ALU.max))
            nc.vector.tensor_tensor(rt[:, 0, :, :], lg, across(rs[:, 0, :]), ALU.subtract).then_inc(centred, 1)
            dve.wait_ge(ld_sel, 32)
            nc.vector.tensor_copy(sel_sb[:, 0:1024], sel_f)
            nc.vector.tensor_copy(sel_sb[:, 1024:NFR * P], sel_f2[:, 0:NFR * P - 1024])
            dve.wait_ge(exped, 1)
            p = rt[:, 1, :, :]
            link(nc.vector.tensor_reduce(rs[:, 1, :], p, AX_X, ALU.add))
            link(nc.vector.reciprocal(rs[:, 2, :], rs[:, 1, :]))
            link(nc.vector.tensor_tensor(p, p, across(rs[:, 2, :]), ALU.mult))
            ranks = rank_sb[:].unsqueeze(1).broadcast_to([P, NT, E])
            for w in range(2):
                top, hit = rs[:, 3 + w, :], rt[:, 2 + w, :, :]
                link(nc.vector.tensor_reduce(top, p, AX_X, ALU.max))
                link(nc.vector.tensor_tensor(hit, p, across(top), ALU.is_equal))
                link(nc.vector.tensor_tensor(hit, hit, ranks, ALU.mult))
                link(nc.vector.tensor_reduce(rs[:, 5, :], hit, AX_X, ALU.max))
                link(nc.vector.tensor_tensor(hit, hit, across(rs[:, 5, :]), ALU.is_equal))
                if w == 0:
                    link(nc.vector.scalar_tensor_tensor(out=p, in0=hit, scalar=-4.0, in1=p, op0=ALU.mult, op1=ALU.add))
                link(nc.vector.tensor_tensor(hit, hit, across(top), ALU.mult))
            link(nc.vector.tensor_tensor(rs[:, 6, :], rs[:, 3, :], rs[:, 4, :], ALU.add))
            link(nc.vector.tensor_scalar(rs[:, 6, :], rs[:, 6, :], 1e-20, None, ALU.add))
            link(nc.vector.reciprocal(rs[:, 7, :], rs[:, 6, :]))
            cw = rt[:, 0, :, :]
            link(nc.vector.tensor_tensor(cw, rt[:, 2, :, :], rt[:, 3, :, :], ALU.add))
            link(nc.vector.tensor_tensor(cw, cw, across(rs[:, 7, :]), ALU.mult))
            half = rt[:, 2, :, :].rearrange("p n e -> p (n e)").bitcast(BF16)[:, 0:NT * E].rearrange("p (n e) -> p n e", e=E)
            for j in range(3):
                link(nc.vector.tensor_copy(half, cw))
                for a in range(2):
                    ins = nc.vector.tensor_copy(cw3[:, a, :, j * E:(j + 1) * E], half[:, 8 * a:8 * a + 8, :])
                if j < 2:
                    link(ins)
                    link(nc.vector.tensor_tensor(cw, cw, half, ALU.subtract))
            ins.then_inc(cw_ready, 1)

            def expert_unit(b, k):
                f = FORDER[k]
                n = NF * b + k
                R = frows(f)
                dve.wait_ge(silu_done, n + 1)
                dve.wait_ge(up_ready, n + 1)
                if n >= HRING:
                    dve.wait_ge(y_ready, 2 * ((n - HRING) // NF + 1))
                h_out = hid[0:R, n % HRING, :]
                mid = hmid[n % 2][0:R, :] if f < NFR else h_out
                ins = nc.vector.tensor_tensor(mid, ps_up[n % 2][0:R, :], gact[n % 2][0:R, :], ALU.mult)
                ins.then_inc(up_taken, 1)
                if f < NFR:
                    dve.wait_ge(up_taken, n + 1)
                    dve.wait_ge(cwb_ready, NFR * b + f + 1)
                    ins = nc.vector.tensor_tensor(h_out, ps_cw[(NFR * b + f) % 2][:, :], mid, ALU.mult)
                    ins.then_inc(hid_ready, 1)

            def finish_rows(b, half_):
                dve.wait_ge(y_ready, 2 * b + half_ + 1)
                n0 = b * TILES + 2 * half_
                ins = nc.vector.tensor_tensor(x_sb[:, n0:n0 + 2, :], ps_y[half_][:, :].rearrange("p (t h) -> p t h", t=2),
                                              x_sb[:, n0:n0 + 2, :], ALU.add)
                ins.then_inc(y_taken, 1)
                dve.wait_ge(y_taken, 2 * b + half_ + 1)
                for t in range(2):
                    ins = nc.vector.bn_stats(stats[:, 2 * half_ + t, :], x_sb[:, n0 + t, :])
                link(ins)
                for t in range(2):
                    ins = nc.vector.bn_aggr(mv[:, 2 * half_ + t, :], stats[:, 2 * half_ + t, :])
                if half_:
                    ins.then_inc(stats_ready, 1)

            for b in range(B):
                for k, f in enumerate(FORDER):
                    if b == 0 and f == 0:
                        for q in range(B):
                            dve.wait_ge(ready, GM + q + 1)
                            nc.vector.tensor_copy(cwT[:, q * S:(q + 1) * S], ps_y[q % 2][0:3 * E, :]).then_inc(cwT_ready, 1)
                    expert_unit(b, k)
                    if b > 0 and k == 2:
                        finish_rows(b - 1, 0)
                        finish_rows(b - 1, 1)
                    if b > 0 and k == 8:
                        normalise(b - 1, B + b - 1)
            finish_rows(B - 1, 0)
            finish_rows(B - 1, 1)
            normalise(B - 1, 2 * B - 1)


def kernel(**inputs):
    import numpy as np
    import concourse.bacc as bacc
    from concourse.bass_utils import run_bass_kernel_spmd

    def arr(name):
        return np.asarray(inputs["L0_" + name])

    order = np.array([(c * 8 + half * 4 + h) * D + d
                      for c in range(HC) for half in range(2) for d in range(D) for h in range(HG)])
    row_head = (order[:P] // D)
    inv_freq = (np.float32(1.0) / np.float32(10000.0) ** (np.arange(0, H, 2, dtype=np.float32) / np.float32(H))).astype(np.float32)
    angle = (np.arange(S, dtype=np.float32)[None, :] * inv_freq[order[:P]][:, None]).astype(np.float32)
    blockmask = np.repeat((row_head[:, None] == np.arange(8)[None, :]).astype(np.float32), D + 1, axis=1)
    feature_expert = np.arange(E * F) // F
    select = np.tile((feature_expert[None, :] == np.arange(E)[:, None]).astype(np.float32), (3, 1))
    xs = arr("attn_hidden_states").reshape(B * S, H)

    def stackT(routed, shared):
        return np.concatenate([routed.reshape(E * F, H), shared], axis=0)

    arrays = {
        "x": xs, "xT": xs.T,
        "wqT": arr("attn_Wq")[order].T, "wkT": arr("attn_Wk")[order].T,
        "wvT": arr("attn_Wv").T, "woT": arr("attn_Wo").T,
        "gate": arr("attn_gate").reshape(1, HEADS),
        "cos": np.cos(angle), "sin": np.sin(angle), "blockmask": blockmask,
        "ident": np.eye(P, dtype=np.float32),
        "gwT": arr("ffn_gate_weight").T,
        "rank": np.tile(np.arange(E, 0, -1, dtype=np.float32), (P, 1)),
        "select": select,
        "wgT": stackT(arr("ffn_w_gate"), arr("ffn_sw_gate")).T,
        "wuT": stackT(arr("ffn_w_up"), arr("ffn_sw_up")).T,
        "wdT": np.concatenate([arr("ffn_w_down").transpose(0, 2, 1).reshape(E * F, H), arr("ffn_sw_down").T], axis=0),
    }
    nc = bacc.Bacc("TRN2", target_bir_lowering=False, num_devices=1)
    aps = {}
    for name in list(arrays):
        a = np.ascontiguousarray(arrays[name])
        arrays[name] = a
        aps[name] = nc.dram_tensor(name, a.shape, mybir.dt.from_np(a.dtype), kind="ExternalInput").ap()
    out = nc.dram_tensor("out", (B * S, H), F32, kind="ExternalOutput").ap()
    build_block(nc, out=out, **aps)
    r = run_bass_kernel_spmd(nc, [arrays], core_ids=[0])
    return r.results[0]["out"].reshape(B, S, H)
```

```python
from contextlib import ExitStack

import concourse.bass as bass
import numpy as np
from concourse import mybir

F32 = mybir.dt.float32
BF16 = mybir.dt.bfloat16
F16 = mybir.dt.float16
ALU = mybir.AluOpType
ACT = mybir.ActivationFunctionType
AX_X = mybir.AxisListType.X

P = 128
B, S, H = 4, 512, 256
HEADS, D = 16, 16
TILES = S // P
HC = H // P
HG = 4
GB = HEADS // HG
NG = B * GB
UNITS = HG * TILES
SCALE = D ** -0.5
EPS = 1e-5
PASSES = ((0, 0), (0, 1), (1, 0))
E, F, FS = 8, 176, 352
FALL = E * F + FS
NF = -(-FALL // P)
NFR = E * F // P
Q_PARTS = (0, 0, 0, 1, 1, 2)
K_PARTS = (0, 1, 2, 0, 1, 0)
KS = len(Q_PARTS) * D
RING = 6
LAG = 2
PAIRS = RING // 2
STACK_INC = 16 * 2 * len(Q_PARTS)
NFS = NF - NFR
HRING = RING * HG
WSCALE = 256.0
WPIECES = 4
ROUNDS = (range(0, B - 1), range(B - 1, B))

FEATURES = [(b, f) for b in range(B) for f in [*range(NFR, NF), *range(NFR)]]
EARLY_AT = [(NG + 2, v) for v in (3, 5, 8, 10, 12, 14)] + [(NG + 3, v) for v in (0, 4, 6, 8, 11, 14)] + [(NG + 4, v) for v in (2, 5, 9)]
EARLY = len(EARLY_AT)


def routed_index(n):
    b, f = FEATURES[n]
    return b * NFR + f


def frows(f):
    return min(P, FALL - f * P)


def stages(i, u):
    out = []
    if i == -1:
        return [(n, 0) for n in (
            "q0", "q1", "rotate_q", "split1_q.0", "split1_q.1", "k0", "resid_q.0", "resid_q.1", "split2_q.0", "split2_q.1",
            "k1", "split3_q.0", "split3_q.1", "rotate_k", "split1_k.0", "split1_k.1", "resid_k.0", "resid_k.1",
            "split2_k.0", "split2_k.1", "split3_k.0", "split3_k.1", "neg_q", "expneg_q", "v0", "v1")] if u == 0 else []
    for b in range(B):
        s, e = (0 if b == 1 else 4 * b - 3), 4 * b + 6
        plan = {
            (s, 0): ["q0"], (s, 2): ["q1", "rotate_q"], (s, 5): ["split1_q", "resid_q"], (s, 8): ["k0", "split2_q", "split3_q"],
            (s, 10): ["k1", "rotate_k"], (s, 9): ["neg_q"], (s, 11): ["expneg_q"],
            (s, 14): ["split1_k", "resid_k"],
            (s + 1, 2): ["split2_k", "split3_k"], (s + 1, 5): ["v0"], (s + 1, 7): ["v1"],
            (s + 1, 13): ["kt0"], (s + 1, 15): ["kt1"],
            (s + 2, 13): ["memory"],
            (s + 3, 5): ["mem0"], (s + 3, 7): ["mem1"], (s + 3, 13): ["mem2"], (s + 3, 15): ["mem3"],
        }
        feats = {(s, 12): ["feat_q"], (s + 1, 1): ["neg_k"], (s + 1, 4): ["expneg_k"], (s + 1, 6): ["feat_k"]}
        if b == 1:
            feats = {(1, 3): ["feat_q"], (1, 4): ["neg_k"], (1, 6): ["expneg_k"], (1, 8): ["feat_k"]}
        if b == 0:
            plan = {(0, 5): ["kt0"], (0, 6): ["kt1"], (0, 11): ["memory"], (0, 13): ["mem0"], (0, 14): ["mem1"],
                    (0, 15): ["mem2"], (1, 1): ["mem3"]}
            feats = {(0, 0): ["feat_q", "neg_k"], (0, 1): ["expneg_k"], (0, 3): ["feat_k"]}
        after = {
            (e, 9): ["ct0"], (e, 11): ["ct1"], (e, 13): ["wo0"], (e, 15): ["wo1"],
            (e + 1, 2): ["ln_sqrt"], (e + 1, 5): ["ln_apply"],
            (e + 1, 10): ["xt0"], (e + 1, 12): ["xt1"], (e + 1, 13): ["x_high", "logits"],
        }
        for p in (plan, feats, after):
            out += [(n, b) for n in p.get((i, u), ())]
    for w, (i_high, at_high, i_low, at_low) in enumerate((
            (NG - 3, (3, 7, 11, 15), NG - 2, (1, 5, 9, 13)),
            (NG - 1, (5, 8, 11, 14), NG, (0, 1, 3, 7)),
            (NG + 4, (4, 6, 8, 10), NG + 4, (5, 7, 9, 11)))):
        for p in range(WPIECES):
            if (i, u) == (i_high, at_high[p]):
                out.append(("w_high", (w, p)))
            if (i, u) == (i_low, at_low[p]):
                out.append(("w_low", (w, p)))
    routing = {(NG, 8): [("centre", 0)], (NG, 10): [("expert_exp", 0)], (NG, 12): [("weigh", 0)],
               (NG + 1, 8): [("cwt", 0)], (NG + 1, 10): [("cwt", 1)], (NG + 1, 12): [("cwt", 2)],
               (NG + 4, 0): [("centre", 1), ("expert_exp", 1)], (NG + 4, 3): [("weigh", 1)], (NG + 4, 12): [("cwt", 3)]}
    out += routing.get((i, u), [])
    if u == 2 and 0 <= i - 1 < NG:
        out.append(("maxt", i - 1))
    if u == 4 and 0 <= i - LAG - 1 < NG:
        out.append(("o_out", i - LAG - 1))
    if u == 6 and 0 <= i - LAG - 1 < NG:
        out.append(("ot", i - LAG - 1))
    if (i, u) in EARLY_AT:
        out.append(("expert", EARLY_AT.index((i, u))))
    return out


TO_SCALAR = ("v0", "v1", "kt0", "kt1", "ct0", "ct1")
TO_VECTOR = ("q0", "q1", "k0", "k1", "memory", "mem0", "mem1", "mem2", "mem3",
             "wo0", "wo1", "xt0", "xt1", "logits", "maxt", "ot", "cwt")
BANKED = TO_SCALAR + TO_VECTOR
ITERATIONS = range(-1, NG + LAG + 3)


def bank_turns():
    turn = {}
    for i in ITERATIONS:
        for u in range(UNITS):
            for s in stages(i, u):
                if s[0] in BANKED:
                    turn[s] = len(turn)
    return turn


def build_block(nc, x, xT, wqT, wkT, wvT, woT, gate, cos, sin, blockmask, ident, gwT, rank, select,
                wgT, wuT, wdT, out):
    TURN = bank_turns()
    TURNS = sorted(TURN, key=TURN.get)

    def nth(s):
        kind = TO_SCALAR if s[0] in TO_SCALAR else TO_VECTOR
        return sum(x[0] in kind for x in TURNS[:TURN[s] + 1])

    with ExitStack() as ctx:
        def sb(name, shape, dt=F32):
            return ctx.enter_context(nc.sbuf_tensor(name, shape, dt))

        def sem(name):
            return ctx.enter_context(nc.semaphore(name))

        banks = [ctx.enter_context(nc.psum_tensor(f"bank{n}", [P, 512], F32)) for n in range(8)]
        ps_score = banks[0:3]
        ps_max = banks[3:5]
        ps_o = banks[5]
        ps_gen = banks[6:8]
        ps_gate, ps_up, ps_cw, ps_y = banks[0:2], banks[2:4], banks[4:6], banks[6:8]

        xT_sb = sb("xT_sb", [P, B, HC, S])
        xpair = [xT_sb[:, b, :, :].rearrange("p c t -> p (c t)").bitcast(F16).rearrange("p (j c t) -> p j c t", j=2, c=HC)
                 for b in range(B)]
        xt32 = sb("xt32", [P, HC, S])
        x_sb = sb("x_sb", [P, B * TILES, H])
        wq_sb, wk_sb, wv_sb, wo_sb = (sb(n, [P, HC, H]) for n in ("wq_sb", "wk_sb", "wv_sb", "wo_sb"))
        cs_sb = sb("cs_sb", [P, 2, S])
        mask_sb = sb("mask_sb", [P, 8, D + 1])
        ident_sb = sb("ident_sb", [P, P])
        gmix = sb("gmix", [P, 4, HEADS])
        eps_sb = sb("eps_sb", [P, 1])
        work = sb("work", [P, 7168])
        prod = work[:, 0:2048].rearrange("p (k t) -> p k t", k=4)
        rot = [work[:, 2048 + 1024 * t:3072 + 1024 * t].rearrange("p (c t) -> p c t", c=HC) for t in range(2)]
        part = [[work[:, 4096 + 512 * (3 * t + j):4608 + 512 * (3 * t + j)].bitcast(BF16)
                 .rearrange("p (c t) -> p c t", c=HC) for j in range(3)] for t in range(2)]
        wpair = [work[:, 2 * FALL * w:2 * FALL * (w + 1)].bitcast(F16).rearrange("p (j n) -> p j n", j=2)
                 for w in range(2)]
        wg_sb, wu_sb = (w.rearrange("p j (c f) -> p j c f", c=HC) for w in wpair)
        linear = sb("linear", [P, 4 * HC * S])
        resid, neg, feat_k = (linear[:, 1024 * n:1024 * (n + 1)].rearrange("p (c t) -> p c t", c=HC) for n in range(3))
        kf_tok = linear[:, 3072:4096].rearrange("p (t f) -> p t f", t=TILES)
        w_raw = linear
        feat = [sb("feat_q", [P, HC, S])[:, :, :], feat_k]
        cwT = feat[0][0:3 * E, :, :].rearrange("p c t -> p (c t)").bitcast(BF16)
        mem_bd = sb("mem_bd", [P, 2, HC, 8 * (D + 1)])
        mem_tok = sb("mem_tok", [P, 2, TILES, H])
        rden = sb("rden", [P, 2, HC, 8])
        stack = sb("stack", [P, 2 * RING * HG * S], BF16)
        qk = stack[:, :].rearrange("p (w r h t) -> p w r h t", r=RING, w=2, h=HG)
        hid = stack[:, :].bitcast(F16).rearrange("p (n j t) -> p n j t", j=2, t=S)
        v_sb = sb("v_sb", [P, 2, TILES, HEADS, 2 * D])
        probs_w = sb("probs_w", [P, 8 * S])
        probs = probs_w[:, :].rearrange("p (n t) -> p n t", n=8)
        wpair.append(probs_w[:, 0:NF * H].bitcast(F16).rearrange("p (j n) -> p j n", j=2))
        wd_sb = wpair[2].rearrange("p j (f n) -> p j f n", f=NF)
        mx = sb("mx", [P, 2, UNITS])
        mneg = sb("mneg", [UNITS, 2, P])
        mres = sb("mres", [UNITS, P])
        mpart = [sb(f"mpart{j}", [UNITS, 2, P], BF16) for j in range(3)]
        o_sb = sb("o_sb", [P, 2, S])
        rsum = sb("rsum", [P, 2, TILES, HG])
        c_tok = sb("c_tok", [P, TILES, H])
        ct_sb = sb("ct_sb", [P, HC, S])
        stats = sb("stats", [P, TILES, 6])
        mv = sb("mv", [P, TILES, 2])
        std = sb("std", [P, 2, TILES])
        NT = B * TILES
        gw_sb = sb("gw_sb", [P, HC, E])
        rank_sb = sb("rank_sb", [P, E])
        lg_sb = sb("lg_sb", [P, NT, E])
        sel_sb = sb("sel_sb", [3 * E, NFR * P], BF16)
        free_tok = mem_tok[:, 0, :, :].rearrange("p t f -> p (t f)")
        rt = free_tok[:, 0:4 * NT * E].rearrange("p (k n e) -> p k n e", k=4, n=NT)
        rs = free_tok[:, 4 * NT * E:4 * NT * E + 8 * NT].rearrange("p (k n) -> p k n", k=8)
        cw3 = free_tok[:, 4 * NT * E + 8 * NT:4 * NT * E + (8 + 3 * E) * NT].rearrange("p (n j) -> p n j", j=3 * E)
        after_v = v_sb[:, :, :, :, :].rearrange("p a t h d -> p (a t h d)")
        gact, hmid, hfull = ([after_v[:, S * (2 * k + n):S * (2 * k + n + 1)] for n in range(2)] for k in range(3))

        ld_q = sem("ld_q"); ld_k = sem("ld_k"); ld_v = sem("ld_v"); ld_ident = sem("ld_ident"); ld_cs = sem("ld_cs")
        ld_x = [sem(f"ld_x{b}") for b in range(B)]
        ld_small = sem("ld_small"); ld_late = sem("ld_late")
        ld_w = [sem(f"ld_w{n}") for n in range(3)]; w_high = sem("w_high"); w_low = sem("w_low")
        ready = sem("ready")
        taken_v = sem("taken_v")
        taken_a = sem("taken_a")
        x_high = sem("x_high"); x_low = sem("x_low")
        max_ready = sem("max_ready"); max_taken = sem("max_taken")
        score_ready = sem("score_ready"); exp_done = sem("exp_done")
        pv_done = sem("pv_done"); o_taken = sem("o_taken")
        rotated = sem("rotated")
        split1 = sem("split1"); resid_ready = sem("resid_ready"); split2 = sem("split2"); split3 = sem("split3")
        neg_ready = sem("neg_ready"); expneg = sem("expneg"); feat_ready = sem("feat_ready")
        stacked = [sem(f"stacked{r}") for r in range(PAIRS)]
        mneg_split = sem("mneg_split"); maxed = [sem(f"maxed{r}") for r in range(2)]
        sigm = sem("sigm"); ones_ready = sem("ones_ready"); init_v = sem("init_v"); init_p = sem("init_p")
        stats_ready = sem("stats_ready"); std_ready = sem("std_ready"); normed = sem("normed")
        vch = sem("vch"); pch = sem("pch")
        centred = sem("centred"); exped = sem("exped")
        cw_ready = sem("cw_ready")
        gate_ready = sem("gate_ready"); up_ready = sem("up_ready"); cwb_ready = sem("cwb_ready")
        silu_done = sem("silu_done"); hid_ready = sem("hid_ready"); up_taken = sem("up_taken")
        hid_high = sem("hid_high"); hid_low = sem("hid_low")
        y_ready = sem("y_ready"); y_taken = sem("y_taken")
        stored = sem("stored")

        def w_blocks(w):
            n = 2 * FALL if w < 2 else (NF - 1) * H
            edges = [n * p // WPIECES for p in range(WPIECES + 1)]
            blocks = [[(P, slice(lo, hi))] for lo, hi in zip(edges, edges[1:])]
            if w == 2:
                blocks[-1].append((frows(NF - 1), slice((NF - 1) * H, NF * H)))
            return blocks

        def split_step(of, b):
            w = int(of[0] == "k")
            cs = slice(int(of[2]), int(of[2]) + 1) if "." in of else slice(0, HC)
            return w, cs, HC * (2 * b + w) + cs.stop

        def rotate(eng, nc_eng, b, w):
            k = 2 * b + w
            after_turn(eng, ("k1" if w else "q1", b))
            if b > 0:
                eng.wait_ge(feat_ready, k - 1)
            nc_eng.tensor_tensor(rot[w][:, 0, :], prod[:, 0, :], prod[:, 2, :], ALU.subtract)
            nc_eng.tensor_tensor(rot[w][:, 1, :], prod[:, 3, :], prod[:, 1, :], ALU.add).then_inc(rotated, 1)

        def first_rest(eng, nc_eng, of, b):
            w, cs, done = split_step(of, b)
            eng.wait_ge(split1, done)
            if 2 * b + w > 0:
                eng.wait_ge(split3, done - HC)
            nc_eng.tensor_tensor(resid[:, cs, :], rot[w][:, cs, :], part[w][0][:, cs, :], ALU.subtract)\
                .then_inc(resid_ready, cs.stop - cs.start)

        def third_part(eng, nc_eng, of, b):
            w, cs, done = split_step(of, b)
            eng.wait_ge(split2, done)
            nc_eng.tensor_tensor(part[w][2][:, cs, :], resid[:, cs, :], part[w][1][:, cs, :], ALU.subtract)\
                .then_inc(split3, cs.stop - cs.start)

        def slots():
            for i in ITERATIONS:
                for u in range(UNITS):
                    yield i, u

        def after_stack(eng, G):
            pair = G // 2
            eng.wait_ge(stacked[pair % PAIRS], STACK_INC * (pair // PAIRS + 1))

        def after_turn(eng, s):
            eng.wait_ge(taken_a if s[0] in TO_SCALAR else taken_v, nth(s))

        block = ctx.enter_context(nc.Block())

        @block.sync
        def _(sp):
            def load_xT(b):
                sp.dma_start(xT_sb[:, b, :, :], xT[:, b * S:(b + 1) * S].rearrange("(c p) t -> p c t", p=P)).then_inc(ld_x[b], 16)

            sp.dma_start(wq_sb[:], wqT.rearrange("(c p) n -> p c n", p=P)).then_inc(ld_q, 16)
            load_xT(0)
            sp.dma_start(cs_sb[:, 0, :], cos).then_inc(ld_cs, 16)
            sp.dma_start(cs_sb[:, 1, :], sin).then_inc(ld_cs, 16)
            sp.dma_start(wk_sb[:], wkT.rearrange("(c p) n -> p c n", p=P)).then_inc(ld_k, 16)
            sp.dma_start(wv_sb[:], wvT.rearrange("(c p) n -> p c n", p=P)).then_inc(ld_v, 16)
            sp.dma_start(ident_sb[:], ident).then_inc(ld_ident, 16)
            load_xT(1)
            sp.dma_start(gmix[:, 0, :], gate.broadcast_to([P, HEADS])).then_inc(ld_small, 16)
            sp.dma_start(mask_sb[:], blockmask.rearrange("p (h d) -> p h d", h=8)).then_inc(ld_small, 16)

            def stack_pair(pair):
                b, c = pair // HC, pair % HC
                if pair >= PAIRS:
                    sp.wait_ge(score_ready, 2 * UNITS * (pair - PAIRS + 1))
                r = 2 * (pair % PAIRS)
                for w, parts in ((0, Q_PARTS), (1, K_PARTS)):
                    for n, j in sorted(enumerate(parts), key=lambda x: x[1]):
                        sp.wait_ge((split1, split2, split3)[j], HC * (2 * b + w) + c + 1)
                        sp.dma_start(qk[n * D:(n + 1) * D, w, r:r + 2, :, :], part[w][j][:, c, :])\
                            .then_inc(stacked[pair % PAIRS], 16)

            stack_pair(0)
            stack_pair(1)
            for dst, src in ((wo_sb[:], woT.rearrange("(c p) n -> p c n", p=P)),
                             (x_sb[:], x.rearrange("(n p) h -> p n h", p=P)),
                             (gw_sb[:], gwT.rearrange("(c p) n -> p c n", p=P)),
                             (rank_sb[:], rank), (sel_sb[:], select)):
                sp.dma_start(dst, src).then_inc(ld_late, 16)
            for b in range(2, B):
                load_xT(b)
            for i in range(1, NG + 1):
                G = i - 1
                sp.wait_ge(mneg_split, G + 1)
                for j in range(3):
                    sp.dma_start(qk[KS + j:KS + j + 1, 0, G % RING, :, :], mpart[j][:, G % 2, :])\
                        .then_inc(maxed[G % 2], 16)
                if i % 2 == 0 and GB <= i + 2 < NG:
                    stack_pair((i + 2) // 2)
                if i == NG - 4:
                    sp.wait_ge(ready, TURN[("memory", B - 1)] + 1)
                    sp.wait_ge(split3, HC * 2 * B)
                    sp.wait_ge(feat_ready, 2 * B)
                    sp.dma_start(w_raw[:, 0:2 * FALL].rearrange("p (c f) -> p c f", c=HC),
                                 wgT.rearrange("(c p) f -> p c f", p=P)).then_inc(ld_w[0], 16)
                if i == NG - 2:
                    sp.wait_ge(w_low, WPIECES)
                    sp.dma_start(w_raw[:, 0:2 * FALL].rearrange("p (c f) -> p c f", c=HC),
                                 wuT.rearrange("(c p) f -> p c f", p=P)).then_inc(ld_w[1], 16)
            sp.wait_ge(w_low, 2 * WPIECES)
            rd = w_raw[:, 0:NF * H].rearrange("p (f n) -> p f n", f=NF)
            sp.dma_start(rd[:, 0:NF - 1, :], wdT[0:(NF - 1) * P, :].rearrange("(f p) n -> p f n", p=P)).then_inc(ld_w[2], 16)
            sp.dma_start(rd[0:frows(NF - 1), NF - 1, :], wdT[(NF - 1) * P:FALL, :]).then_inc(ld_w[2], 16)
            for b in range(B - 1):
                sp.wait_ge(normed, B + b + 1)
                sp.dma_start(out[b * S:(b + 1) * S, :].rearrange("(n p) h -> p n h", p=P),
                             x_sb[:, b * TILES:(b + 1) * TILES, :]).then_inc(stored, 16)
            for n in range((B - 1) * TILES, B * TILES):
                sp.wait_ge(normed, 2 * B - 1 + n - (B - 1) * TILES + 1)
                sp.dma_start(out[n * P:(n + 1) * P, :], x_sb[:, n, :]).then_inc(stored, 16)
            sp.wait_ge(stored, 16 * (B - 1 + TILES))

        @block.tensor
        def _(pe):
            def open_turn(s):
                n = TURN[s]
                if n >= 2:
                    after_turn(pe, TURNS[n - 2])
                return ps_gen[n % 2]

            def project(dst, w, b, c):
                for k in range(HC):
                    ins = nc.tensor.matmul(dst[:, 0:S], w[:, k, c * P:(c + 1) * P],
                                           xT_sb[:, b, k, :], start=(k == 0), stop=(k == HC - 1))
                return ins

            def banked(s):
                name, b = s
                g = open_turn(s)
                kind, n = name.rstrip("0123"), int(name[-1]) if name[-1].isdigit() else 0
                if kind == "q":
                    if b == 0 and n == 0:
                        pe.wait_ge(ld_q, 16)
                    if n == 0:
                        pe.wait_ge(ld_x[b], 16)
                    ins = project(g, wq_sb, b, n)
                elif kind == "k":
                    if b == 0 and n == 0:
                        pe.wait_ge(ld_k, 16)
                    ins = project(g, wk_sb, b, n)
                elif kind == "v":
                    if b == 0 and n == 0:
                        pe.wait_ge(ld_v, 16)
                    for t in range(2):
                        t0 = (2 * n + t) * P
                        for k in range(HC):
                            ins = nc.tensor.matmul(g[:, t * H:(t + 1) * H], xT_sb[:, b, k, t0:t0 + P], wv_sb[:, k, :],
                                                   start=(k == 0), stop=(k == HC - 1))
                elif kind == "kt":
                    if b == 0 and n == 0:
                        pe.wait_ge(ld_ident, 16)
                    pe.wait_ge(feat_ready, 2 * b + 2)
                    for t in range(2):
                        for c in range(HC):
                            o = (t * HC + c) * P
                            t0 = (2 * n + t) * P
                            ins = nc.tensor.transpose(g[:, o:o + P], feat[1][:, c, t0:t0 + P], ident_sb[:])
                elif kind == "memory":
                    after_turn(pe, ("kt1", b))
                    after_turn(pe, ("v1", b))
                    for c in range(HC):
                        for t in range(TILES):
                            ins = nc.tensor.matmul(g[:, c * 136:c * 136 + 136], kf_tok[:, t, c * P:(c + 1) * P],
                                                   v_sb[:, b % 2, t, 8 * c:8 * c + 8, 0:D + 1],
                                                   start=(t == 0), stop=(t == TILES - 1))
                elif kind == "mem":
                    after_turn(pe, ("memory", b))
                    pe.wait_ge(feat_ready, 2 * b + 1)
                    for c in range(HC):
                        ins = nc.tensor.matmul(g[:, c * 136:c * 136 + 136], feat[0][:, c, n * P:(n + 1) * P],
                                               mem_bd[:, b % 2, c, :], start=True, stop=True)
                elif kind == "maxt":
                    pe.wait_ge(max_taken, UNITS * (b + 1))
                    ins = nc.tensor.transpose(g[0:UNITS, 0:P], mx[:, b % 2, :], ident_sb[:])
                elif kind == "ot":
                    pe.wait_ge(o_taken, b + 1)
                    for t in range(TILES):
                        ins = nc.tensor.transpose(g[:, t * P:(t + 1) * P], o_sb[:, b % 2, t * P:(t + 1) * P], ident_sb[:])
                elif kind == "ct":
                    after_turn(pe, ("ot", GB * b + GB - 1))
                    for c in range(HC):
                        for t in range(2):
                            o = (c * 2 + t) * P
                            ins = nc.tensor.transpose(g[:, o:o + P], c_tok[:, 2 * n + t, c * P:(c + 1) * P], ident_sb[:])
                elif kind == "wo":
                    after_turn(pe, (f"ct{n}", b))
                    if b == 0 and n == 0:
                        pe.wait_ge(ld_late, 16 * 5)
                    for t in range(2):
                        for c in range(HC):
                            ins = nc.tensor.matmul(g[:, t * H:(t + 1) * H], ct_sb[:, c, (2 * n + t) * P:(2 * n + t + 1) * P],
                                                   wo_sb[:, c, :], start=(c == 0), stop=(c == HC - 1))
                elif kind == "xt":
                    pe.wait_ge(normed, b + 1)
                    for c in range(HC):
                        for t in range(2):
                            o = (c * 2 + t) * P
                            ins = nc.tensor.transpose(g[:, o:o + P], x_sb[:, b * TILES + 2 * n + t, c * P:(c + 1) * P],
                                                      ident_sb[:])
                elif kind == "cwt":
                    pe.wait_ge(cw_ready, 1 if b in ROUNDS[0] else 2)
                    for t in range(TILES):
                        ins = nc.tensor.transpose(g[0:3 * E, t * P:(t + 1) * P], cw3[:, b * TILES + t, :], ident_sb[:])
                elif kind == "logits":
                    after_turn(pe, ("xt1", b))
                    for t in range(TILES):
                        for c in range(HC):
                            ins = nc.tensor.matmul(g[:, t * E:(t + 1) * E], xt32[:, c, t * P:(t + 1) * P], gw_sb[:, c, :],
                                                   start=(c == 0), stop=(c == HC - 1))
                ins.then_inc(ready, 1)

            def feature_chunk(n):
                b, f = FEATURES[n]
                R = frows(f)
                if n == 0:
                    pe.wait_ge(w_low, 2 * WPIECES)
                if f == NFR:
                    pe.wait_ge(x_low, b + 1)
                if n >= 2:
                    pe.wait_ge(silu_done, n - 1)
                for dst, w, s in ((ps_gate[n % 2], wg_sb, gate_ready), (ps_up[n % 2], wu_sb, up_ready)):
                    if s is up_ready and n >= 2:
                        pe.wait_ge(up_taken, n - 1)
                    for c in range(HC):
                        for p, (jw, jx) in enumerate(PASSES):
                            ins = nc.tensor.matmul(dst[0:R, :], w[:, jw, c, f * P:f * P + R], xpair[b][:, jx, c, :],
                                                   start=(c == 0 and p == 0), stop=(c == HC - 1 and p == 2))
                    ins.then_inc(s, 1)
                if f < NFR:
                    m = routed_index(n)
                    if f == 0:
                        after_turn(pe, ("cwt", b))
                    if m == 1:
                        pe.wait_ge(o_taken, NG)
                    if m >= 2:
                        pe.wait_ge(hid_ready, m - 1)
                    nc.tensor.matmul(ps_cw[m % 2][:, :], sel_sb[:, f * P:(f + 1) * P], cwT[:, b * S:(b + 1) * S],
                                     start=True, stop=True).then_inc(cwb_ready, 1)

            def value_product(m):
                G, t = m // TILES, m % TILES
                b = G // GB
                pe.wait_ge(exp_done, HG * (m + 1))
                if t == 0:
                    if G % GB == 0:
                        after_turn(pe, ("v1", b))
                    if G >= 1:
                        pe.wait_ge(o_taken, G)
                for h in range(HG):
                    ins = nc.tensor.matmul(ps_o[32 * h:32 * h + 32, :], v_sb[:, b % 2, t, (G % GB) * HG + h, :],
                                           probs[:, (HG * m + h) % 8, :], start=(t == 0), stop=(t == TILES - 1))
                ins.then_inc(pv_done, 1)

            for i, u in slots():
                t, h = u // HG, u % HG
                if 0 <= i < NG:
                    if u == 0:
                        after_stack(pe, i)
                    n = UNITS * i + u
                    if n >= 2:
                        pe.wait_ge(max_taken, n - 1)
                    nc.tensor.matmul(ps_max[n % 2][:, :], qk[0:KS, 0, i % RING, h, t * P:(t + 1) * P],
                                     qk[0:KS, 1, i % RING, h, :], start=True, stop=True).then_inc(max_ready, 1)
                j = i - LAG
                if 0 <= j < NG:
                    if u == 0:
                        pe.wait_ge(maxed[j % 2], 48 * (j // 2 + 1))
                        if j == 0:
                            pe.wait_ge(ones_ready, 1)
                    n = UNITS * j + u
                    if n >= 3:
                        pe.wait_ge(exp_done, n - 2)
                    nc.tensor.matmul(ps_score[n % 3][:, :], qk[0:KS + 3, 1, j % RING, h, t * P:(t + 1) * P],
                                     qk[0:KS + 3, 0, j % RING, h, :], start=True, stop=True).then_inc(score_ready, 1)
                m = (UNITS * j + u - 6) // HG
                if (UNITS * j + u - 6) % HG == 0 and 0 <= m < NG * TILES:
                    value_product(m)
                for s in stages(i, u):
                    if s[0] in BANKED:
                        banked(s)
                    if s[0] == "expert":
                        feature_chunk(s[1])

            def down(b):
                if b == 0:
                    pe.wait_ge(w_low, 3 * WPIECES)
                pe.wait_ge(hid_low, NF * (b + 1))
                for t in range(TILES):
                    if b == B - 1:
                        dst = banks[(6, 7, 4, 5)[t]][:, 0:H]
                        if t < 2:
                            pe.wait_ge(y_taken, TILES * b - 2 + 2 * t)
                    else:
                        dst = ps_y[t // 2][:, (t % 2) * H:(t % 2 + 1) * H]
                        if t == 0:
                            if b == 0:
                                after_turn(pe, TURNS[-1])
                            else:
                                pe.wait_ge(y_taken, TILES * b)
                    for n in range(NF * b, NF * (b + 1)):
                        f = FEATURES[n][1]
                        R = frows(f)
                        for p, (jh, jw) in enumerate(PASSES):
                            ins = nc.tensor.matmul(dst, hid[0:R, n % HRING, jh, t * P:(t + 1) * P], wd_sb[0:R, jw, f, :],
                                                   start=(n == NF * b and p == 0), stop=(n == NF * (b + 1) - 1 and p == 2))
                    ins.then_inc(y_ready, 1)

            for n in range(EARLY, len(FEATURES)):
                feature_chunk(n)
                if n >= NF and n % NF == 1:
                    down(n // NF - 1)
            down(B - 1)

        @block.scalar
        def _(act):
            def banked(s):
                name, b = s
                g = ps_gen[TURN[s] % 2]
                kind, n = name.rstrip("0123"), int(name[-1])
                act.wait_ge(ready, TURN[s] + 1)
                if kind == "v":
                    if b == 0 and n == 0:
                        act.wait_ge(init_p, 1)
                    if b >= 2:
                        act.wait_ge(pv_done, GB * TILES * (b - 1))
                    dst, src = v_sb[:, b % 2, 2 * n:2 * n + 2, :, 0:D], g[:, :].rearrange("p (t h d) -> p t h d", t=2, h=HEADS)
                if kind == "kt":
                    dst, src = kf_tok[:, 2 * n:2 * n + 2, :], g[:, :].rearrange("p (t f) -> p t f", t=2)
                if kind == "ct":
                    dst, src = ct_sb[:, :, 2 * n * P:(2 * n + 2) * P], g[:, :].rearrange("p (c t) -> p c t", c=HC)
                nc.scalar.activation(dst, src, ACT.Copy).then_inc(taken_a, 1)

            def feature_chunk(n):
                R = frows(FEATURES[n][1])
                act.wait_ge(gate_ready, n + 1)
                if n >= 2:
                    act.wait_ge(up_taken, n - 1)
                elif n == 0:
                    act.wait_ge(pv_done, NG * TILES)
                nc.scalar.activation(gact[n % 2][0:R, :], ps_gate[n % 2][0:R, :], ACT.Silu, scale=1.0 / WSCALE)\
                    .then_inc(silu_done, 1)
                if n >= 1:
                    high_part(n - 1)

            def high_part(n):
                b, f = FEATURES[n]
                R = frows(f)
                if n == 0:
                    act.wait_ge(score_ready, NG * UNITS)
                if f >= NFR:
                    act.wait_ge(up_taken, n + 1)
                else:
                    act.wait_ge(hid_ready, routed_index(n) + 1)
                if n >= HRING:
                    act.wait_ge(y_ready, TILES * ((n - HRING) // NF + 1))
                nc.scalar.activation(hid[0:R, n % HRING, 0, :], hfull[n % 2][0:R, :], ACT.Copy).then_inc(hid_high, 1)

            for i, u in slots():
                j = i - LAG
                if 0 <= j < NG:
                    n = UNITS * j + u
                    act.wait_ge(score_ready, n + 1)
                    if n >= 8:
                        act.wait_ge(pv_done, n // HG - 1)
                    nc.scalar.activation(probs[:, n % 8, :], ps_score[n % 3][:, :], ACT.Exp, scale=SCALE)\
                        .then_inc(exp_done, 1)
                for s in stages(i, u):
                    name, b = s
                    if name in TO_SCALAR:
                        banked(s)
                    if name == "mem0" and b == 0:
                        act.wait_ge(ld_small, 32)
                        nc.scalar.activation(gmix[:, 1, :], gmix[:, 0, :], ACT.Exp, scale=-1.0).then_inc(sigm, 1)
                    if name == "o_out":
                        act.wait_ge(pv_done, TILES * (b + 1))
                        if b >= 2:
                            act.wait_ge(ready, TURN[("ot", b - 2)] + 1)
                        nc.scalar.activation(o_sb[:, b % 2, :], ps_o[:, :], ACT.Copy).then_inc(o_taken, 1)
                    if name == "ln_sqrt":
                        after_turn(act, ("wo1", b))
                        act.wait_ge(init_v, 1)
                        nc.scalar.activation(std[:, 0, :], mv[:, :, 1], ACT.Sqrt, bias=eps_sb[:, 0:1])\
                            .then_inc(std_ready, 1)
                    if name == "x_high":
                        after_turn(act, ("xt1", b))
                        nc.scalar.activation(xpair[b][:, 0, :, :], xt32[:], ACT.Copy).then_inc(x_high, 1)
                    if name == "w_high":
                        w, p = b
                        if p == 0:
                            act.wait_ge(ld_w[w], 16 if w < 2 else 32)
                        if w == 0 and p == 0:
                            for G in range(NG - GB, NG):
                                after_stack(act, G)
                        if w == 2 and p == 0:
                            act.wait_ge(pv_done, NG * TILES)
                        for rows, cols in w_blocks(w)[p]:
                            ins = nc.scalar.activation(wpair[w][0:rows, 0, cols], w_raw[0:rows, cols], ACT.Copy, scale=WSCALE)
                        ins.then_inc(w_high, 1)
                    if name == "expert_exp":
                        act.wait_ge(centred, b + 1)
                        n0, n1 = ROUNDS[b][0] * TILES, (ROUNDS[b][-1] + 1) * TILES
                        nc.scalar.activation(rt[:, 1, n0:n1, :], rt[:, 0, n0:n1, :], ACT.Exp).then_inc(exped, 1)
                    if name == "expert":
                        feature_chunk(b)
                    kind, _, of = name.partition("_")
                    if kind in ("split1", "split2", "expneg"):
                        w, cs, done = split_step(of, b)
                        k = 2 * b + w
                        if kind == "split1":
                            act.wait_ge(rotated, k + 1)
                            if b > 0:
                                for c in range(HC):
                                    after_stack(act, GB * (b - 1) + 2 * c)
                            nc.scalar.activation(part[w][0][:, cs, :], rot[w][:, cs, :], ACT.Copy).then_inc(split1, cs.stop - cs.start)
                        if kind == "split2":
                            act.wait_ge(resid_ready, done)
                            nc.scalar.activation(part[w][1][:, cs, :], resid[:, cs, :], ACT.Copy).then_inc(split2, cs.stop - cs.start)
                        if kind == "expneg":
                            act.wait_ge(neg_ready, k + 1)
                            nc.scalar.activation(neg, neg, ACT.Exp).then_inc(expneg, 1)

            for n in range(EARLY, len(FEATURES)):
                feature_chunk(n)
                if n >= NF and n % NF == 6:
                    act.wait_ge(stats_ready, n // NF)
                    nc.scalar.activation(std[:, 0, :], mv[:, :, 1], ACT.Sqrt, bias=eps_sb[:, 0:1]).then_inc(std_ready, 1)
            high_part(len(FEATURES) - 1)
            for t in range(TILES):
                act.wait_ge(stats_ready, B + t)
                nc.scalar.activation(std[:, 0, t:t + 1], mv[:, t, 1:2], ACT.Sqrt, bias=eps_sb[:, 0:1]).then_inc(std_ready, 1)

        @block.gpsimd
        def _(pool):
            nc.gpsimd.memset(v_sb[:], 1.0).then_inc(init_p, 1)
            pool.wait_ge(init_p, 1)
            chain = [0]

            def link(ins):
                chain[0] += 1
                ins.then_inc(pch, 1)
                pool.wait_ge(pch, chain[0])

            def rest(n):
                R = frows(FEATURES[n][1])
                pool.wait_ge(hid_high, n + 1)
                nc.gpsimd.tensor_tensor(hid[0:R, n % HRING, 1, :], hfull[n % 2][0:R, :], hid[0:R, n % HRING, 0, :],
                                        ALU.subtract).then_inc(hid_low, 1)

            for i, u in slots():
                for name, b in stages(i, u):
                    if name == "expert" and b > 0:
                        rest(b - 1)
                    kind, _, of = name.partition("_")
                    if kind == "rotate" and b > 0:
                        rotate(pool, nc.gpsimd, b, int(of == "k"))
                    if kind == "resid" and b > 0:
                        first_rest(pool, nc.gpsimd, of, b)
                    if kind == "split3" and b > 0:
                        third_part(pool, nc.gpsimd, of, b)
                    if name == "maxt":
                        G = b
                        after_turn(pool, ("maxt", G))
                        if G >= 2:
                            pool.wait_ge(maxed[G % 2], 48 * (G // 2))
                        m, pt = mneg[:, G % 2, :], [x[:, G % 2, :] for x in mpart]
                        link(nc.gpsimd.tensor_copy(pt[0], m))
                        link(nc.gpsimd.tensor_tensor(mres[:], m, pt[0], ALU.subtract))
                        link(nc.gpsimd.tensor_copy(pt[1], mres[:]))
                        nc.gpsimd.tensor_tensor(pt[2], mres[:], pt[1], ALU.subtract).then_inc(mneg_split, 1)
                    if name == "x_high":
                        pool.wait_ge(x_high, b + 1)
                        nc.gpsimd.tensor_tensor(xpair[b][:, 1, :, :], xt32[:], xpair[b][:, 0, :, :], ALU.subtract)\
                            .then_inc(x_low, 1)

            for n in range(EARLY - 1, len(FEATURES)):
                rest(n)

        @block.vector
        def _(dve):
            chain = [0]

            def link(ins):
                chain[0] += 1
                ins.then_inc(vch, 1)
                dve.wait_ge(vch, chain[0])

            ones2 = float(np.frombuffer(np.array([0x3F80, 0x3F80], np.uint16).tobytes(), np.float32)[0])
            ones_rows = stack[KS:KS + 3, RING * HG * S:].bitcast(F32)
            nc.vector.memset(ones_rows, ones2).then_inc(ones_ready, 1)
            link(nc.vector.memset(eps_sb[:], EPS))
            nc.vector.memset(std[:], 1.0).then_inc(init_v, 1)

            def banked(s):
                name, b = s
                g = ps_gen[TURN[s] % 2]
                kind, n = name.rstrip("0123"), int(name[-1]) if name[-1].isdigit() else 0
                dve.wait_ge(ready, TURN[s] + 1)
                if kind in ("q", "k"):
                    k = 2 * b + int(kind == "k")
                    if k == 0 and n == 0:
                        dve.wait_ge(ld_cs, 32)
                    if k > 0 and n == 0:
                        dve.wait_ge(rotated, k)
                    nc.vector.tensor_tensor(prod[:, 2 * n, :] if n == 0 else prod[:, 3, :], g[:, :], cs_sb[:, 0, :], ALU.mult)
                    ins = nc.vector.tensor_tensor(prod[:, 1, :] if n == 0 else prod[:, 2, :], g[:, :], cs_sb[:, 1, :], ALU.mult)
                elif kind == "memory":
                    for c in range(HC):
                        ins = nc.vector.tensor_tensor(mem_bd[:, b % 2, c, :].rearrange("p (h d) -> p h d", h=8),
                                                      g[:, c * 136:c * 136 + 136].rearrange("p (h d) -> p h d", h=8),
                                                      mask_sb[:], ALU.mult)
                elif kind == "mem":
                    gv = g[:, 0:HC * 136].rearrange("p (c h d) -> p c h d", c=HC, h=8)
                    link(nc.vector.reciprocal(rden[:, 0, :, :], gv[:, :, :, D]))
                    link(nc.vector.tensor_tensor(rden[:, 1, :, :], rden[:, 0, :, :],
                                                 gmix[:, 2, :].rearrange("p (c h) -> p c h", c=HC), ALU.mult))
                    for c in range(HC):
                        ins = nc.vector.tensor_tensor(
                            mem_tok[:, b % 2, n, c * P:(c + 1) * P].rearrange("p (h d) -> p h d", h=8),
                            gv[:, c, :, 0:D], rden[:, 1, c, :].unsqueeze(2).broadcast_to([P, 8, D]), ALU.mult)
                elif kind == "maxt":
                    if b >= 2:
                        dve.wait_ge(mneg_split, b - 1)
                    ins = nc.vector.tensor_scalar(mneg[:, b % 2, :], g[0:UNITS, 0:P], -1.0, None, ALU.mult)
                elif kind == "ot":
                    G, bb = b, b // GB
                    gv = g[:, :].rearrange("p (t h d) -> p t h d", t=TILES, h=HG)
                    h0 = (G % GB) * HG
                    link(nc.vector.reciprocal(rsum[:, 0, :, :], gv[:, :, :, D]))
                    link(nc.vector.tensor_tensor(rsum[:, 1, :, :], rsum[:, 0, :, :],
                                                 gmix[:, 3, h0:h0 + HG].unsqueeze(1).broadcast_to([P, TILES, HG]), ALU.mult))
                    if G % GB == 0 and bb > 0:
                        dve.wait_ge(ready, TURN[("ct1", bb - 1)] + 1)
                    for t in range(TILES):
                        ins = nc.vector.tensor_tensor(
                            c_tok[:, t, h0 * D:(h0 + HG) * D].rearrange("p (h d) -> p h d", h=HG),
                            gv[:, t, :, 0:D], rsum[:, 1, t, :].unsqueeze(2).broadcast_to([P, HG, D]), ALU.mult)
                    link(ins)
                    cv = c_tok[:, :, h0 * D:(h0 + HG) * D]
                    ins = nc.vector.tensor_tensor(cv, cv, mem_tok[:, bb % 2, :, h0 * D:(h0 + HG) * D], ALU.add)
                elif kind == "wo":
                    n0 = b * TILES + 2 * n
                    link(nc.vector.tensor_tensor(x_sb[:, n0:n0 + 2, :], g[:, :].rearrange("p (t h) -> p t h", t=2),
                                                 x_sb[:, n0:n0 + 2, :], ALU.add))
                    for t in range(2):
                        ins = nc.vector.bn_stats(stats[:, 2 * n + t, :], x_sb[:, n0 + t, :])
                    link(ins)
                    for t in range(2):
                        ins = nc.vector.bn_aggr(mv[:, 2 * n + t, :], stats[:, 2 * n + t, :])
                elif kind == "xt":
                    if b > 0 and n == 0:
                        dve.wait_ge(x_low, b)
                        dve.wait_ge(ready, TURN[("logits", b - 1)] + 1)
                    ins = nc.vector.tensor_copy(xt32[:, :, 2 * n * P:(2 * n + 2) * P],
                                                g[:, :].rearrange("p (c t) -> p c t", c=HC))
                elif kind == "cwt":
                    ins = nc.vector.tensor_copy(cwT[:, b * S:(b + 1) * S], g[0:3 * E, :])
                elif kind == "logits":
                    ins = nc.vector.tensor_copy(lg_sb[:, b * TILES:(b + 1) * TILES, :],
                                                g[:, 0:TILES * E].rearrange("p (t e) -> p t e", e=E))
                ins.then_inc(taken_v, 1)

            def normalise(b, k):
                dve.wait_ge(std_ready, k + 1)
                link(nc.vector.reciprocal(std[:, 1, :], std[:, 0, :]))
                for t in range(TILES):
                    row = x_sb[:, b * TILES + t, :]
                    ins = nc.vector.tensor_scalar(row, row, mv[:, t, 0:1], std[:, 1, t:t + 1], ALU.subtract, ALU.mult)
                ins.then_inc(normed, 1)

            def feature_chunk(n):
                b, f = FEATURES[n]
                R = frows(f)
                dve.wait_ge(silu_done, n + 1)
                dve.wait_ge(up_ready, n + 1)
                if n >= 2:
                    dve.wait_ge(hid_low, n - 1)
                full = hfull[n % 2][0:R, :]
                if f >= NFR:
                    nc.vector.scalar_tensor_tensor(out=full, in0=ps_up[n % 2][0:R, :], scalar=1.0 / WSCALE,
                                                   in1=gact[n % 2][0:R, :], op0=ALU.mult, op1=ALU.mult).then_inc(up_taken, 1)
                    return
                m = routed_index(n)
                nc.vector.tensor_tensor(hmid[n % 2][:, :], ps_up[n % 2][:, :], gact[n % 2][:, :], ALU.mult).then_inc(up_taken, 1)
                dve.wait_ge(up_taken, n + 1)
                dve.wait_ge(cwb_ready, m + 1)
                nc.vector.tensor_tensor(full, ps_cw[m % 2][:, :], hmid[n % 2][:, :], ALU.mult).then_inc(hid_ready, 1)

            def across(a):
                return a.unsqueeze(2).broadcast_to([P, a.shape[1], E])

            def tiles_of(r):
                return slice(ROUNDS[r][0] * TILES, (ROUNDS[r][-1] + 1) * TILES)

            def centre(r):
                N = tiles_of(r)
                dve.wait_ge(taken_v, nth(("logits", ROUNDS[r][-1])))
                link(nc.vector.tensor_reduce(rs[:, 0, N], lg_sb[:, N, :], AX_X, ALU.max))
                nc.vector.tensor_tensor(rt[:, 0, N, :], lg_sb[:, N, :], across(rs[:, 0, N]), ALU.subtract).then_inc(centred, 1)

            def weigh(r):
                N = tiles_of(r)
                dve.wait_ge(exped, r + 1)
                p = rt[:, 1, N, :]
                link(nc.vector.tensor_reduce(rs[:, 1, N], p, AX_X, ALU.add))
                link(nc.vector.reciprocal(rs[:, 2, N], rs[:, 1, N]))
                link(nc.vector.tensor_tensor(p, p, across(rs[:, 2, N]), ALU.mult))
                ranks = rank_sb[:].unsqueeze(1).broadcast_to([P, N.stop - N.start, E])
                for w in range(2):
                    top, hit = rs[:, 3 + w, N], rt[:, 2 + w, N, :]
                    link(nc.vector.tensor_reduce(top, p, AX_X, ALU.max))
                    link(nc.vector.tensor_tensor(hit, p, across(top), ALU.is_equal))
                    link(nc.vector.tensor_tensor(hit, hit, ranks, ALU.mult))
                    link(nc.vector.tensor_reduce(rs[:, 5, N], hit, AX_X, ALU.max))
                    link(nc.vector.tensor_tensor(hit, hit, across(rs[:, 5, N]), ALU.is_equal))
                    if w == 0:
                        link(nc.vector.scalar_tensor_tensor(out=p, in0=hit, scalar=-4.0, in1=p, op0=ALU.mult, op1=ALU.add))
                    link(nc.vector.tensor_tensor(hit, hit, across(top), ALU.mult))
                link(nc.vector.tensor_tensor(rs[:, 6, N], rs[:, 3, N], rs[:, 4, N], ALU.add))
                link(nc.vector.tensor_scalar(rs[:, 6, N], rs[:, 6, N], 1e-20, None, ALU.add))
                link(nc.vector.reciprocal(rs[:, 7, N], rs[:, 6, N]))
                cw = rt[:, 0, N, :]
                link(nc.vector.tensor_tensor(cw, rt[:, 2, N, :], rt[:, 3, N, :], ALU.add))
                link(nc.vector.tensor_tensor(cw, cw, across(rs[:, 7, N]), ALU.mult))
                half = rt[:, 2, N, :].rearrange("p n e -> p (n e)").bitcast(BF16)[:, 0:(N.stop - N.start) * E]\
                    .rearrange("p (n e) -> p n e", e=E)
                for j in range(3):
                    link(nc.vector.tensor_copy(half, cw))
                    ins = nc.vector.tensor_copy(cw3[:, N, j * E:(j + 1) * E], half)
                    if j < 2:
                        link(ins)
                        link(nc.vector.tensor_tensor(cw, cw, half, ALU.subtract))
                ins.then_inc(cw_ready, 1)

            for i, u in slots():
                if 0 <= i < NG:
                    n = UNITS * i + u
                    t, h = u // HG, u % HG
                    dve.wait_ge(max_ready, n + 1)
                    if u == 0 and i >= 2:
                        dve.wait_ge(ready, TURN[("maxt", i - 2)] + 1)
                    nc.vector.tensor_reduce(mx[:, i % 2, h * TILES + t:h * TILES + t + 1], ps_max[n % 2][:, :], AX_X, ALU.max)\
                        .then_inc(max_taken, 1)
                for s in stages(i, u):
                    name, b = s
                    if name in TO_VECTOR:
                        if s == ("memory", 0):
                            dve.wait_ge(ld_small, 32)
                        if s == ("wo0", 0):
                            dve.wait_ge(ld_late, 16 * 5)
                        if s == ("mem0", 0):
                            dve.wait_ge(sigm, 1)
                            link(nc.vector.tensor_scalar(gmix[:, 2, :], gmix[:, 1, :], 1.0, None, ALU.add))
                            link(nc.vector.reciprocal(gmix[:, 2, :], gmix[:, 2, :]))
                            link(nc.vector.tensor_scalar(gmix[:, 3, :], gmix[:, 2, :], -1.0, 1.0, ALU.mult, ALU.add))
                        banked(s)
                    if name in ("feat_q", "feat_k"):
                        w = int(name[-1] == "k")
                        dve.wait_ge(expneg, 2 * b + w + 1)
                        dve.wait_ge(rotated, 2 * b + w + 1)
                        if b > 0:
                            dve.wait_ge(ready, TURN[("kt1" if w else "mem3", b - 1)] + 1)
                        nc.vector.scalar_tensor_tensor(out=feat[w], in0=rot[w], scalar=0.0, in1=neg,
                                                       op0=ALU.max, op1=ALU.add).then_inc(feat_ready, 1)
                    kind, _, of = name.partition("_")
                    if kind == "rotate" and b == 0:
                        rotate(dve, nc.vector, b, int(of == "k"))
                    if kind == "resid" and b == 0:
                        first_rest(dve, nc.vector, of, b)
                    if kind == "split3" and b == 0:
                        third_part(dve, nc.vector, of, b)
                    if kind == "neg":
                        k = 2 * b + int(of == "k")
                        dve.wait_ge(rotated, k + 1)
                        if k > 0:
                            dve.wait_ge(feat_ready, k)
                        nc.vector.tensor_scalar(neg, rot[k % 2], 0.0, None, ALU.min).then_inc(neg_ready, 1)
                    if name == "ln_apply":
                        normalise(b, b)
                    if name == "w_low":
                        w, p = b
                        dve.wait_ge(w_high, WPIECES * w + p + 1)
                        for rows, cols in w_blocks(w)[p]:
                            ins = nc.vector.scalar_tensor_tensor(
                                out=wpair[w][0:rows, 1, cols], in0=w_raw[0:rows, cols], scalar=WSCALE,
                                in1=wpair[w][0:rows, 0, cols], op0=ALU.mult, op1=ALU.subtract)
                        ins.then_inc(w_low, 1)
                    if name == "centre":
                        centre(b)
                    if name == "weigh":
                        weigh(b)
                    if name == "expert":
                        feature_chunk(b)

            def finish_tile(b, t):
                n = b * TILES + t
                dve.wait_ge(y_ready, n + 1)
                y = banks[(6, 7, 4, 5)[t]][:, 0:H] if b == B - 1 else ps_y[t // 2][:, (t % 2) * H:(t % 2 + 1) * H]
                nc.vector.scalar_tensor_tensor(out=x_sb[:, n, :], in0=y, scalar=1.0 / WSCALE, in1=x_sb[:, n, :],
                                               op0=ALU.mult, op1=ALU.add).then_inc(y_taken, 1)
                dve.wait_ge(y_taken, n + 1)
                link(nc.vector.bn_stats(stats[:, t, :], x_sb[:, n, :]))
                ins = nc.vector.bn_aggr(mv[:, t, :], stats[:, t, :])
                if t == TILES - 1 or b == B - 1:
                    ins.then_inc(stats_ready, 1)

            for n in range(EARLY, len(FEATURES)):
                b, k = n // NF, n % NF
                if b > 0 and k == 2:
                    for t in range(TILES):
                        if t % 2 == 0:
                            dve.wait_ge(y_ready, (b - 1) * TILES + t + 2)
                        finish_tile(b - 1, t)
                feature_chunk(n)
                if b > 0 and k == 7:
                    normalise(b - 1, B + b - 1)
            for t in range(TILES):
                finish_tile(B - 1, t)
                dve.wait_ge(std_ready, 2 * B + t)
                link(nc.vector.reciprocal(std[:, 1, t:t + 1], std[:, 0, t:t + 1]))
                row = x_sb[:, (B - 1) * TILES + t, :]
                nc.vector.tensor_scalar(row, row, mv[:, t, 0:1], std[:, 1, t:t + 1], ALU.subtract, ALU.mult).then_inc(normed, 1)


def kernel(**inputs):
    import concourse.bacc as bacc
    import ml_dtypes
    from concourse.bass_utils import run_bass_kernel_spmd

    def arr(name):
        return np.asarray(inputs["L0_" + name])

    order = np.array([(c * 8 + h) * D + d
                      for c in range(HC) for d in range(D) for h in range(8)])
    row_head = (order[:P] // D)
    inv_freq = (np.float32(1.0) / np.float32(10000.0) ** (np.arange(0, H, 2, dtype=np.float32) / np.float32(H))).astype(np.float32)
    angle = (np.arange(S, dtype=np.float32)[None, :] * inv_freq[order[:P]][:, None]).astype(np.float32)
    blockmask = np.repeat((row_head[:, None] == np.arange(8)[None, :]).astype(np.float32), D + 1, axis=1)
    feature_expert = np.arange(E * F) // F
    select = (np.tile(feature_expert[None, :] == np.arange(E)[:, None], (3, 1)) / WSCALE).astype(ml_dtypes.bfloat16)
    xs = arr("attn_hidden_states").reshape(B * S, H)

    def stackT(routed, shared):
        return np.concatenate([routed.reshape(E * F, H), shared], axis=0)

    arrays = {
        "x": xs, "xT": xs.T,
        "wqT": arr("attn_Wq")[order].T, "wkT": arr("attn_Wk")[order].T,
        "wvT": arr("attn_Wv").T, "woT": arr("attn_Wo").T,
        "gate": arr("attn_gate").reshape(1, HEADS),
        "cos": np.cos(angle), "sin": np.sin(angle), "blockmask": blockmask,
        "ident": np.eye(P, dtype=np.float32),
        "gwT": arr("ffn_gate_weight").T,
        "rank": np.tile(np.arange(E, 0, -1, dtype=np.float32), (P, 1)),
        "select": select,
        "wgT": stackT(arr("ffn_w_gate"), arr("ffn_sw_gate")).T,
        "wuT": stackT(arr("ffn_w_up"), arr("ffn_sw_up")).T,
        "wdT": np.concatenate([arr("ffn_w_down").transpose(0, 2, 1).reshape(E * F, H), arr("ffn_sw_down").T], axis=0),
    }
    nc = bacc.Bacc("TRN2", target_bir_lowering=False, num_devices=1)
    aps = {}
    for name in list(arrays):
        a = np.ascontiguousarray(arrays[name])
        arrays[name] = a
        aps[name] = nc.dram_tensor(name, a.shape, mybir.dt.from_np(a.dtype), kind="ExternalInput").ap()
    out = nc.dram_tensor("out", (B * S, H), F32, kind="ExternalOutput").ap()
    build_block(nc, out=out, **aps)
    r = run_bass_kernel_spmd(nc, [arrays], core_ids=[0])
    return r.results[0]["out"].reshape(B, S, H)
```

```python
from contextlib import ExitStack

import concourse.bass as bass
import numpy as np
from concourse import mybir

F32 = mybir.dt.float32
BF16 = mybir.dt.bfloat16
F16 = mybir.dt.float16
ALU = mybir.AluOpType
ACT = mybir.ActivationFunctionType
AX_X = mybir.AxisListType.X

P = 128
B, S, H = 4, 512, 256
HEADS, D = 16, 16
TILES = S // P
HC = H // P
HG = 4
GB = HEADS // HG
NG = B * GB
UNITS = HG * TILES
SCALE = D ** -0.5
EPS = 1e-5
PASSES = ((0, 0), (0, 1), (1, 0))
E, F, FS = 8, 176, 352
FALL = E * F + FS
NF = -(-FALL // P)
NFR = E * F // P
Q_PARTS = (0, 0, 0, 1, 1, 2)
K_PARTS = (0, 1, 2, 0, 1, 0)
KS = len(Q_PARTS) * D
RING = 6
LAG = 32
VALUE_LAG = 6
PAIRS = RING // 2
STACK_INC = 16 * 2 * len(Q_PARTS)
HRING = RING * HG
WSCALE = 256.0
SCORE_RING = 2
MAX_RING = 5 - SCORE_RING
LATE_FOR_SCALAR = ("k1", "kt1", "ct1",)
LATE_FOR_VECTOR = ("xt1",)
CW_RING = 4
PAIRED = 2
WPIECES = 4
ROUNDS = (range(0, B - 1), range(B - 1, B))

FEATURES = [(b, f) for b in range(B) for f in [*range(NFR, NF), *range(NFR)]]
EARLY_AT = [
    (18, 4), (18, 4), (18, 7), (18, 11), (18, 11), (19, 3), (19, 3), (19, 8), (19, 10), (20, 3), (20, 5), (20, 5),
    (20, 8), (20, 12), (20, 15),
]
EARLY = len(EARLY_AT)


def experts_of(f):
    return [(e, max(0, e * F - f * P), min(P, (e + 1) * F - f * P)) for e in range(f * P // F, (f * P + P - 1) // F + 1)]


def cw_loads(m):
    return sum(len(experts_of(k % NFR)) for k in range(m % CW_RING, m + 1, CW_RING))


def routed_index(n):
    b, f = FEATURES[n]
    return b * NFR + f


def frows(f):
    return min(P, FALL - f * P)


PROJECT = {
    "xs_high.0": (-1, 13), "xs_high.1": (0, 2), "xs_low": (0, 3), "q0": (0, 12), "q1": (0, 12), "rotate_q": (0, 15),
    "exp_q.0": (1, 4), "k0": (1, 5), "split1_q.0": (1, 5), "split1_q.1": (1, 7), "resid_q": (1, 7),
    "split2_q.0": (1, 11), "k1": (1, 12), "split2_q.1": (1, 12), "split3_q.0": (1, 14), "split3_q.1": (1, 14),
    "rotate_k": (2, 1), "exp_q.1": (2, 4), "v0": (2, 4), "split1_k.0": (2, 6), "relu_q.0": (2, 8),
    "relu_q.1": (2, 9), "feat_q": (2, 10), "exp_k.0": (2, 11), "exp_k.1": (2, 13), "relu_k.0": (2, 14),
    "relu_k.1": (2, 15), "split1_k.1": (3, 0), "feat_k": (3, 0), "resid_k": (3, 5), "v1": (3, 6),
    "split2_k.0": (3, 7), "split3_k.0": (3, 9), "kt0": (3, 9), "kt1": (4, 4), "split2_k.1": (4, 5),
    "split3_k.1": (4, 8), "memory": (4, 8), "mem0": (4, 13), "mem1": (5, 0), "mem2": (5, 3), "mem3": (5, 4),
}
PROJECT_SECOND = {
    "q0": (1, 10), "q1": (1, 12), "rotate_q": (2, 1), "split1_q.0": (2, 2), "split1_q.1": (2, 3), "resid_q": (2, 3),
    "k0": (2, 5), "exp_q.0": (2, 5), "split2_q.0": (2, 6), "split3_q.0": (2, 7), "k1": (2, 9), "split3_q.1": (2, 10),
    "split2_q.1": (2, 13), "v0": (2, 13), "rotate_k": (2, 15), "exp_q.1": (3, 0), "relu_q.0": (3, 1),
    "relu_q.1": (3, 4), "split1_k.0": (3, 6), "split1_k.1": (3, 7), "feat_q": (3, 8), "resid_k": (3, 11),
    "split2_k.0": (3, 12), "split3_k.0": (3, 13), "exp_k.0": (3, 14), "exp_k.1": (4, 0), "relu_k.0": (4, 0),
    "relu_k.1": (4, 2), "split2_k.1": (4, 3), "feat_k": (4, 4), "v1": (4, 4), "split3_k.1": (4, 6), "kt0": (4, 8),
    "kt1": (4, 13), "memory": (5, 9), "mem0": (5, 11), "mem1": (5, 15), "mem2": (6, 0), "mem3": (6, 3),
}
BEFORE = (
    "cos_q0", "sin_q1", "sum_q.0", "q0", "split1_q.0", "q1", "cos_k0", "k0", "resid_q.0", "sin_k1", "sum_k.0",
    "split2_q.0", "split1_k.0", "k1", "split3_q.0", "v0", "resid_k.0", "split2_k.0", "v1", "cos_q1", "sin_q0",
    "sum_q.1", "exp_q", "split3_k.0", "sin_k0", "relu_q", "cos_k1", "sum_k.1", "split1_k.1", "split1_q.1",
)
PROJECT_FIRST = {
    "feat_q": (3, 4), "resid_q.1": (3, 6), "split2_q.1": (3, 7), "split3_q.1": (3, 8), "resid_k.1": (3, 15),
    "exp_k": (3, 15), "relu_k": (4, 8), "feat_k": (4, 9), "split2_k.1": (4, 10), "split3_k.1": (4, 13),
    "kt0": (4, 14), "kt1": (4, 15), "memory": (5, 1), "mem0": (5, 1), "mem1": (5, 6), "mem2": (5, 12),
    "mem3": (6, 0),
}
FINISH = {
    "ct0": (0, 11), "ct1": (0, 13), "wo0": (0, 13), "wo1": (1, 1), "ln_sqrt": (1, 4), "ln_apply": (1, 6),
    "xt0": (1, 12), "x_high0": (1, 14), "xt1": (2, 0), "x_high1": (3, 3), "logits": (3, 8),
}
FINISH_THIRD = {
    "ct0": (0, 11), "ct1": (0, 13), "wo0": (1, 1), "wo1": (1, 1), "ln_sqrt": (1, 4), "ln_apply": (1, 6),
    "xt0": (1, 11), "x_high0": (1, 12), "xt1": (1, 12), "logits": (2, 0), "x_high1": (4, 3),
}
FINISH_LAST = {
    "ct0": (0, 10), "ct1": (0, 12), "wo0": (0, 12), "wo1": (1, 1), "ln_sqrt": (1, 2), "ln_apply": (1, 2),
    "xt0": (1, 4), "xt1": (1, 9), "logits": (1, 11), "x_high0": (2, 0), "x_high1": (2, 10),
}
MAXT = (1, 2)
GROUP = {
    "o_out": (1, 2), "ot": (1, 7),
}
WEIGHTS = {
    ("w_high", 0): ((13, 6), (13, 10), (13, 12), (14, 5)), ("w_low", 0): ((13, 13), (14, 3), (14, 14), (14, 15)),
    ("w_high", 1): ((15, 14), (16, 2), (16, 5), (16, 13)), ("w_low", 1): ((16, 6), (16, 12), (16, 12), (17, 9)),
    ("w_high", 2): ((20, 2), (20, 4), (20, 6), (20, 6)), ("w_low", 2): ((20, 4), (20, 6), (20, 6), (20, 14)),
}
PROJECTION_WEIGHTS = {
    ("pw_high", 0): (-1, 10), ("pw_low", 0): (0, 5), ("pw_high", 1): (1, 1), ("pw_low", 1): (3, 3),
    ("pw_high", 2): (3, 4), ("pw_low", 2): (4, 2),
}
ROUTING = {
    ("centre", 0): (16, 0), ("expert_exp", 0): (16, 2), ("weigh", 0): (16, 3), ("cwt", 0): (17, 12),
    ("cwt", 1): (17, 15), ("cwt", 2): (17, 15), ("centre", 1): (19, 15), ("expert_exp", 1): (20, 3),
    ("weigh", 1): (20, 3), ("cwt", 3): (20, 9),
}


def timetable():
    table = {(-1, 0): [(name, 0) for name in BEFORE]}

    def put(iteration, unit, *stage):
        table.setdefault((iteration + unit // UNITS, unit % UNITS), []).append(stage)

    for b in range(B):
        for name, (i, u) in (PROJECT_FIRST, PROJECT_SECOND, PROJECT, PROJECT)[b].items():
            put(max(4 * (b - 1) - (b == 1), -4) + i, u, name, b)
        for name, (i, u) in (FINISH, FINISH, FINISH_THIRD, FINISH_LAST)[b].items():
            put(4 * b + 4 + i, LAG + u, name, b)
    for (name, w), places in WEIGHTS.items():
        for p, (i, u) in enumerate(places):
            put(i, u, name, (w, p))
    for (name, r), (i, u) in (PROJECTION_WEIGHTS | ROUTING).items():
        put(i, u, name, r)
    for G in range(NG):
        put(G + MAXT[0], MAXT[1], "maxt", G)
        for name, (i, u) in GROUP.items():
            put(G + i, LAG + u, name, G)
    for n, (i, u) in enumerate(EARLY_AT):
        put(i, u, "expert", n)
    return table


def stages(i, u):
    return TIMETABLE.get((i, u), [])


ROPED = ("q0", "q1", "k0", "k1")
TO_SCALAR = ("v0", "v1", "kt0", "kt1", "ct0", "ct1")
TO_VECTOR = ("memory", "mem0", "mem1", "mem2", "mem3",
             "wo0", "wo1", "xt0", "xt1", "logits", "maxt", "ot", "cwt")


def banked_stage(s):
    return s[0] in TO_SCALAR + TO_VECTOR or s[0] in ROPED and s[1] > 0
ITERATIONS = range(-1, NG + 5)


def max_bank(m):
    return m % 5 if m < LAG else SCORE_RING + m % MAX_RING


def score_bank(n):
    tail = NG * UNITS - LAG
    if n < tail:
        return n % SCORE_RING
    order = [max_bank(NG * UNITS - MAX_RING + k) for k in range(MAX_RING)] + [(tail + k) % SCORE_RING for k in range(SCORE_RING)]
    return order[(n - tail) % 5]


def last_use(bank_of, n, bank):
    return max([k + 1 for k in range(max(0, n - 6), n) if bank_of(k) == bank], default=0)


def to_scalar(s):
    return s[0] in TO_SCALAR or s[0] in ROPED and s[1] > 0


TIMETABLE = timetable()


def bank_turns():
    turn = {}
    for i in ITERATIONS:
        for u in range(UNITS):
            for s in stages(i, u):
                if banked_stage(s):
                    turn[s] = len(turn)
    return turn


def build_block(nc, x, xT, wqT, wkT, wvT, woT, gate, cos, sin, blockmask, ident, gwT, rank, cw_dram,
                wgT, wuT, wdT, out):
    TURN = bank_turns()
    TURNS = sorted(TURN, key=TURN.get)

    def nth(s):
        return sum(to_scalar(x) == to_scalar(s) for x in TURNS[:TURN[s] + 1])

    with ExitStack() as ctx:
        def sb(name, shape, dt=F32):
            return ctx.enter_context(nc.sbuf_tensor(name, shape, dt))

        def sem(name):
            return ctx.enter_context(nc.semaphore(name))

        banks = [ctx.enter_context(nc.psum_tensor(f"bank{n}", [P, 512], F32)) for n in range(8)]
        ps_o = banks[5]
        ps_gen = banks[6:8]
        ps_gate, ps_up, ps_y = banks[0:2], banks[2:4], banks[6:8]

        xT_sb = sb("xT_sb", [P, B, HC, S])
        xpair = [xT_sb[:, b, :, :].rearrange("p c t -> p (c t)").bitcast(F16).rearrange("p (j c t) -> p j c t", j=2, c=HC)
                 for b in range(B)]
        xt32 = sb("xt32", [P, HC, S])
        x_sb = sb("x_sb", [P, B * TILES, H])
        wq_sb, wk_sb, wv_sb, wo_sb = (sb(n, [P, HC, H]) for n in ("wq_sb", "wk_sb", "wv_sb", "wo_sb"))
        pq_sb = sb("pq_sb", [P, HC * H])
        w32 = [w[:, :, :].rearrange("p c n -> p (c n)") for w in (wq_sb, wk_sb, wv_sb)]
        wproj = [w.bitcast(F16).rearrange("p (j c n) -> p j c n", j=2, c=HC) for w in (pq_sb[:, :], w32[0], w32[1])]
        cs_sb = sb("cs_sb", [P, 2, S])
        mask_sb = sb("mask_sb", [P, 8, D + 1])
        ident_sb = sb("ident_sb", [P, P])
        gmix = sb("gmix", [P, 4, HEADS])
        eps_sb = sb("eps_sb", [P, 1])
        work = sb("work", [P, 7168])
        prod = work[:, 0:2048].rearrange("p (k t) -> p k t", k=4)
        rot = [work[:, 2048 + 1024 * t:3072 + 1024 * t].rearrange("p (c t) -> p c t", c=HC) for t in range(2)]
        part = [[work[:, 4096 + 512 * (3 * t + j):4608 + 512 * (3 * t + j)].bitcast(BF16)
                 .rearrange("p (c t) -> p c t", c=HC) for j in range(3)] for t in range(2)]
        wpair = [work[:, 2 * FALL * w:2 * FALL * (w + 1)].bitcast(F16).rearrange("p (j n) -> p j n", j=2)
                 for w in range(2)]
        wg_sb, wu_sb = (w.rearrange("p j (c f) -> p j c f", c=HC) for w in wpair)
        linear = sb("linear", [P, 4 * HC * S])
        resid, exp_r, feat_k = (linear[:, 1024 * n:1024 * (n + 1)].rearrange("p (c t) -> p c t", c=HC) for n in range(3))
        kf_tok = linear[:, 3072:4096].rearrange("p (t f) -> p t f", t=TILES)
        w_raw = linear
        feat = [sb("feat_q", [P, HC, S])[:, :, :], feat_k]
        cwT = feat[0][0:E, :, :]
        mem_bd = sb("mem_bd", [P, 2, HC, 8 * (D + 1)])
        mem_tok = sb("mem_tok", [P, 2, TILES, H])
        rden = sb("rden", [P, 2, HC, 8])
        stack = sb("stack", [P, 2 * RING * HG * S], BF16)
        qk = stack[:, :].rearrange("p (w r h t) -> p w r h t", r=RING, w=2, h=HG)
        hid = stack[:, :].bitcast(F16).rearrange("p (n j t) -> p n j t", j=2, t=S)
        v_sb = sb("v_sb", [P, 2, TILES, HEADS, 2 * D])
        probs_w = sb("probs_w", [P, 8 * S])
        probs = probs_w[:, :].rearrange("p (n t) -> p n t", n=8)
        wpair.append(probs_w[:, 0:NF * H].bitcast(F16).rearrange("p (j n) -> p j n", j=2))
        wd_sb = wpair[2].rearrange("p j (f n) -> p j f n", f=NF)
        mx = sb("mx", [P, 2, UNITS])
        mneg = sb("mneg", [UNITS, 2, P])
        mres = sb("mres", [UNITS, P])
        mpart = [sb(f"mpart{j}", [UNITS, 2, P], BF16) for j in range(3)]
        o_sb = sb("o_sb", [P, 2, S])
        rsum = sb("rsum", [P, 2, TILES, HG])
        c_tok = sb("c_tok", [P, TILES, H])
        ct_sb = sb("ct_sb", [P, HC, S])
        stats = sb("stats", [P, TILES, 6])
        mv = sb("mv", [P, TILES, 2])
        std = sb("std", [P, 2, TILES])
        NT = B * TILES
        gw_sb = sb("gw_sb", [P, HC, E])
        rank_sb = sb("rank_sb", [P, E])
        lg_sb = sb("lg_sb", [P, NT, E])
        free_tok = mem_tok[:, 0, :, :].rearrange("p t f -> p (t f)")
        rt = free_tok[:, 0:4 * NT * E].rearrange("p (k n e) -> p k n e", k=4, n=NT)
        rs = free_tok[:, 4 * NT * E:4 * NT * E + 8 * NT].rearrange("p (k n) -> p k n", k=8)
        after_v = v_sb[:, :, :, :, :].rearrange("p a t h d -> p (a t h d)")
        cw_rows = [mem_tok[:, 1, 2 * n:2 * n + 2, :].rearrange("p t f -> p (t f)") for n in range(2)] + \
            [after_v[:, S * n:S * (n + 1)] for n in (6, 7)]
        gact, hmid, hfull = ([after_v[:, S * (2 * k + n):S * (2 * k + n + 1)] for n in range(2)] for k in range(3))

        ld_q = sem("ld_q"); ld_k = sem("ld_k"); ld_v = sem("ld_v"); ld_ident = sem("ld_ident")
        ld_cs = [sem(f"ld_{n}") for n in ("cos", "sin")]
        ld_x = [sem(f"ld_x{b}") for b in range(B)]
        ld_small = sem("ld_small"); ld_late = sem("ld_late")
        ld_w = [sem(f"ld_w{n}") for n in range(3)]; w_high = sem("w_high"); w_low = sem("w_low")
        pw_high = sem("pw_high"); pw_low = sem("pw_low"); xs_high = sem("xs_high"); xs_low = sem("xs_low")
        ready = sem("ready")
        taken_v = sem("taken_v")
        taken_a = sem("taken_a")
        x_high = sem("x_high"); x_low = sem("x_low")
        max_ready = sem("max_ready"); max_taken = sem("max_taken")
        score_ready = sem("score_ready"); exp_done = sem("exp_done")
        pv_done = sem("pv_done"); o_taken = sem("o_taken")
        first_ready = sem("first_ready"); rotated = [sem(f"rotated_{n}") for n in "qk"]
        split1, resid_ready, split2, split3 = ([sem(f"{kind}_{n}") for n in "qk"]
                                               for kind in ("split1", "resid_ready", "split2", "split3"))
        rope_ready = sem("rope_ready"); elu_parts = sem("elu_parts"); feat_ready = sem("feat_ready")
        stacked = [sem(f"stacked{r}") for r in range(PAIRS)]
        mneg_split = sem("mneg_split"); maxed = [sem(f"maxed{r}") for r in range(2)]
        sigm = sem("sigm"); ones_ready = sem("ones_ready"); init_v = sem("init_v"); init_p = sem("init_p")
        stats_ready = sem("stats_ready"); std_ready = sem("std_ready"); normed = sem("normed")
        vch = sem("vch"); pch = sem("pch")
        centred = sem("centred"); exped = sem("exped")
        cw_ready = sem("cw_ready")
        gate_ready = sem("gate_ready"); up_ready = sem("up_ready")
        cw_stored = [sem(f"cw_stored{n}") for n in range(2)]; cw_loaded = [sem(f"cw_loaded{n}") for n in range(CW_RING)]
        silu_done = sem("silu_done"); hid_ready = sem("hid_ready"); up_taken = sem("up_taken")
        hid_high = sem("hid_high"); hid_low = sem("hid_low")
        y_ready = sem("y_ready"); y_taken = sem("y_taken")
        stored = sem("stored")

        def w_blocks(w):
            n = 2 * FALL if w < 2 else (NF - 1) * H
            edges = [n * p // WPIECES for p in range(WPIECES + 1)]
            blocks = [[(P, slice(lo, hi))] for lo, hi in zip(edges, edges[1:])]
            if w == 2:
                blocks[-1].append((frows(NF - 1), slice((NF - 1) * H, NF * H)))
            return blocks

        def split_step(of, b):
            w = int(of[0] == "k")
            cs = slice(int(of[2]), int(of[2]) + 1) if "." in of else slice(0, HC)
            return w, cs, HC * b + cs.stop

        def rotate(eng, nc_eng, b, w):
            eng.wait_ge(rope_ready, 2 * b + w - 1)
            nc_eng.tensor_tensor(rot[w][:, 0, :], prod[:, 0, :], prod[:, 3, :], ALU.subtract)
            nc_eng.tensor_tensor(rot[w][:, 1, :], prod[:, 1, :], prod[:, 2, :], ALU.add).then_inc(rotated[w], HC)

        def feature(eng, nc_eng, b, w):
            eng.wait_ge(elu_parts, HC * (2 * b + w + 1))
            nc_eng.scalar_tensor_tensor(out=feat[w], in0=exp_r, scalar=1.0, in1=feat[w], op0=ALU.min, op1=ALU.add)\
                .then_inc(feat_ready, 1)

        def first_rest(eng, nc_eng, of, b):
            w, cs, done = split_step(of, b)
            eng.wait_ge(split1[w], done)
            if w == 1:
                eng.wait_ge(split3[0], done)
            elif b > 0:
                eng.wait_ge(split3[1], done - HC)
            nc_eng.tensor_tensor(resid[:, cs, :], rot[w][:, cs, :], part[w][0][:, cs, :], ALU.subtract)\
                .then_inc(resid_ready[w], cs.stop - cs.start)

        def third_part(eng, nc_eng, of, b):
            w, cs, done = split_step(of, b)
            eng.wait_ge(split2[w], done)
            nc_eng.tensor_tensor(part[w][2][:, cs, :], resid[:, cs, :], part[w][1][:, cs, :], ALU.subtract)\
                .then_inc(split3[w], cs.stop - cs.start)

        def to_read(i, u, late):
            n = i * UNITS + u - 1
            before = stages(n // UNITS, n % UNITS) if n >= 0 else []
            return [s for s in before if s[0] in late] + [s for s in stages(i, u) if i < 0 or s[0] not in late]

        def slots():
            for i in ITERATIONS:
                for u in range(UNITS):
                    yield i, u

        def after_stack(eng, G):
            pair = G // 2
            eng.wait_ge(stacked[pair % PAIRS], STACK_INC * (pair // PAIRS + 1))

        def after_turn(eng, s):
            eng.wait_ge(taken_a if to_scalar(s) else taken_v, nth(s))

        block = ctx.enter_context(nc.Block())

        @block.sync
        def _(sp):
            def load_xT(b):
                sp.dma_start(xT_sb[:, b, :, :], xT[:, b * S:(b + 1) * S].rearrange("(c p) t -> p c t", p=P)).then_inc(ld_x[b], 16)

            sp.dma_start(wq_sb[:], wqT.rearrange("(c p) n -> p c n", p=P)).then_inc(ld_q, 16)
            load_xT(0)
            sp.dma_start(cs_sb[:, 0, :], cos).then_inc(ld_cs[0], 16)
            sp.dma_start(cs_sb[:, 1, :], sin).then_inc(ld_cs[1], 16)
            sp.dma_start(wk_sb[:], wkT.rearrange("(c p) n -> p c n", p=P)).then_inc(ld_k, 16)
            sp.dma_start(wv_sb[:], wvT.rearrange("(c p) n -> p c n", p=P)).then_inc(ld_v, 16)
            sp.dma_start(ident_sb[:], ident).then_inc(ld_ident, 16)
            load_xT(1)
            sp.dma_start(gmix[:, 0, :], gate.broadcast_to([P, HEADS])).then_inc(ld_small, 16)
            sp.dma_start(mask_sb[:], blockmask.rearrange("p (h d) -> p h d", h=8)).then_inc(ld_small, 16)

            def stack_pair(pair):
                b, c = pair // HC, pair % HC
                if pair >= PAIRS:
                    sp.wait_ge(score_ready, 2 * UNITS * (pair - PAIRS + 1))
                r = 2 * (pair % PAIRS)
                for w, parts in ((0, Q_PARTS), (1, K_PARTS)):
                    for n, j in sorted(enumerate(parts), key=lambda x: x[1]):
                        sp.wait_ge((split1, split2, split3)[j][w], HC * b + c + 1)
                        sp.dma_start(qk[n * D:(n + 1) * D, w, r:r + 2, :, :], part[w][j][:, c, :])\
                            .then_inc(stacked[pair % PAIRS], 16)

            stack_pair(0)
            stack_pair(1)
            for dst, src in ((wo_sb[:], woT.rearrange("(c p) n -> p c n", p=P)),
                             (x_sb[:], x.rearrange("(n p) h -> p n h", p=P)),
                             (gw_sb[:], gwT.rearrange("(c p) n -> p c n", p=P)),
                             (rank_sb[:], rank)):
                sp.dma_start(dst, src).then_inc(ld_late, 16)
            for b in range(2, B):
                load_xT(b)
            for i in range(1, NG + 1):
                G = i - 1
                sp.wait_ge(mneg_split, G + 1)
                for j in range(3):
                    sp.dma_start(qk[KS + j:KS + j + 1, 0, G % RING, :, :], mpart[j][:, G % 2, :])\
                        .then_inc(maxed[G % 2], 16)
                if i % 2 == 0 and GB <= i + 2 < NG:
                    stack_pair((i + 2) // 2)
                if i == NG - 4:
                    sp.wait_ge(ready, TURN[("memory", B - 1)] + 1)
                    for w in range(2):
                        sp.wait_ge(split3[w], HC * B)
                    sp.wait_ge(feat_ready, 2 * B)
                    sp.dma_start(w_raw[:, 0:2 * FALL].rearrange("p (c f) -> p c f", c=HC),
                                 wgT.rearrange("(c p) f -> p c f", p=P)).then_inc(ld_w[0], 16)
                if i == NG - 2:
                    sp.wait_ge(w_low, WPIECES)
                    sp.dma_start(w_raw[:, 0:2 * FALL].rearrange("p (c f) -> p c f", c=HC),
                                 wuT.rearrange("(c p) f -> p c f", p=P)).then_inc(ld_w[1], 16)
            sp.wait_ge(w_low, 2 * WPIECES)
            rd = w_raw[:, 0:NF * H].rearrange("p (f n) -> p f n", f=NF)
            sp.dma_start(rd[:, 0:NF - 1, :], wdT[0:(NF - 1) * P, :].rearrange("(f p) n -> p f n", p=P)).then_inc(ld_w[2], 16)
            sp.dma_start(rd[0:frows(NF - 1), NF - 1, :], wdT[(NF - 1) * P:FALL, :]).then_inc(ld_w[2], 16)
            def store_weights(b):
                after_turn(sp, ("cwt", b))
                sp.dma_start(cw_dram[:, b * S:(b + 1) * S], cwT[:, b % 2, :]).then_inc(cw_stored[b % 2], 16)

            for n, (b, f) in enumerate(FEATURES):
                if b < B - 1 and n % NF == 0:
                    if b == 0:
                        store_weights(0)
                    if b + 1 < B - 1:
                        store_weights(b + 1)
                if b == B - 2 and n % NF == 4:
                    store_weights(B - 1)
                if f < NFR:
                    m = routed_index(n)
                    if f == 0:
                        sp.wait_ge(cw_stored[b % 2], 16 * (b // 2 + 1))
                    if m == 0:
                        after_turn(sp, ("ot", NG - 1))
                        sp.wait_ge(pv_done, NG * TILES)
                    if m >= CW_RING:
                        sp.wait_ge(hid_ready, m - CW_RING + 1)
                    for e, lo, hi in experts_of(f):
                        sp.dma_start(cw_rows[m % CW_RING][lo:hi, :], cw_dram[e:e + 1, b * S:(b + 1) * S].broadcast_to([hi - lo, S]))\
                            .then_inc(cw_loaded[m % CW_RING], 16)
                if b > 0 and n % NF == NF - 2:
                    sp.wait_ge(normed, B + b)
                    sp.dma_start(out[(b - 1) * S:b * S, :].rearrange("(n p) h -> p n h", p=P),
                                 x_sb[:, (b - 1) * TILES:b * TILES, :]).then_inc(stored, 16)
            for n in range((B - 1) * TILES, B * TILES):
                sp.wait_ge(normed, 2 * B - 1 + n - (B - 1) * TILES + 1)
                sp.dma_start(out[n * P:(n + 1) * P, :], x_sb[:, n, :]).then_inc(stored, 16)
            sp.wait_ge(stored, 16 * (B - 1 + TILES))

        @block.tensor
        def _(pe):
            def open_turn(s):
                n = TURN[s]
                if n >= 2:
                    after_turn(pe, TURNS[n - 2])
                return ps_gen[n % 2]

            def project(dst, w, b, c):
                if b >= PAIRED:
                    pe.wait_ge(pw_low, w + 1)
                    pe.wait_ge(xs_low, b - PAIRED + 1)
                    for k in range(HC):
                        for p, (jw, jx) in enumerate(PASSES):
                            ins = nc.tensor.matmul(dst[:, 0:S], wproj[w][:, jw, k, c * P:(c + 1) * P], xpair[b - 1][:, jx, k, :],
                                                   start=(k == 0 and p == 0), stop=(k == HC - 1 and p == 2))
                    return ins
                w = (wq_sb, wk_sb)[w]
                for k in range(HC):
                    ins = nc.tensor.matmul(dst[:, 0:S], w[:, k, c * P:(c + 1) * P],
                                           xT_sb[:, b, k, :], start=(k == 0), stop=(k == HC - 1))
                return ins

            def first_product(name):
                w, c = int(name[0] == "k"), int(name[-1])
                if c == 0:
                    pe.wait_ge((ld_q, ld_k)[w], 16)
                    pe.wait_ge(ld_x[0], 16)
                project(banks[2 * w + c], w, 0, c).then_inc(first_ready, 1)

            def banked(s):
                name, b = s
                g = open_turn(s)
                kind, n = name.rstrip("0123"), int(name[-1]) if name[-1].isdigit() else 0
                if kind == "q":
                    if n == 0 and b < PAIRED:
                        pe.wait_ge(ld_x[b], 16)
                    ins = project(g, 0, b, n)
                elif kind == "k":
                    ins = project(g, 1, b, n)
                elif kind == "v":
                    if b == 0 and n == 0:
                        pe.wait_ge(ld_v, 16)
                    for t in range(2):
                        t0 = (2 * n + t) * P
                        if b >= PAIRED:
                            pe.wait_ge(pw_low, 3)
                        for k in range(HC):
                            if b >= PAIRED:
                                for p, (jx, jw) in enumerate(PASSES):
                                    ins = nc.tensor.matmul(g[:, t * H:(t + 1) * H], xpair[b - 1][:, jx, k, t0:t0 + P],
                                                           wproj[2][:, jw, k, :],
                                                           start=(k == 0 and p == 0), stop=(k == HC - 1 and p == 2))
                            else:
                                ins = nc.tensor.matmul(g[:, t * H:(t + 1) * H], xT_sb[:, b, k, t0:t0 + P], wv_sb[:, k, :],
                                                       start=(k == 0), stop=(k == HC - 1))
                elif kind == "kt":
                    if b == 0 and n == 0:
                        pe.wait_ge(ld_ident, 16)
                    pe.wait_ge(feat_ready, 2 * b + 2)
                    for t in range(2):
                        for c in range(HC):
                            o = (t * HC + c) * P
                            t0 = (2 * n + t) * P
                            ins = nc.tensor.transpose(g[:, o:o + P], feat[1][:, c, t0:t0 + P], ident_sb[:])
                elif kind == "memory":
                    after_turn(pe, ("kt1", b))
                    after_turn(pe, ("v1", b))
                    for c in range(HC):
                        for t in range(TILES):
                            ins = nc.tensor.matmul(g[:, c * 136:c * 136 + 136], kf_tok[:, t, c * P:(c + 1) * P],
                                                   v_sb[:, b % 2, t, 8 * c:8 * c + 8, 0:D + 1],
                                                   start=(t == 0), stop=(t == TILES - 1))
                elif kind == "mem":
                    after_turn(pe, ("memory", b))
                    pe.wait_ge(feat_ready, 2 * b + 1)
                    for c in range(HC):
                        ins = nc.tensor.matmul(g[:, c * 136:c * 136 + 136], feat[0][:, c, n * P:(n + 1) * P],
                                               mem_bd[:, b % 2, c, :], start=True, stop=True)
                elif kind == "maxt":
                    pe.wait_ge(max_taken, UNITS * (b + 1))
                    ins = nc.tensor.transpose(g[0:UNITS, 0:P], mx[:, b % 2, :], ident_sb[:])
                elif kind == "ot":
                    pe.wait_ge(o_taken, b + 1)
                    for t in range(TILES):
                        ins = nc.tensor.transpose(g[:, t * P:(t + 1) * P], o_sb[:, b % 2, t * P:(t + 1) * P], ident_sb[:])
                elif kind == "ct":
                    after_turn(pe, ("ot", GB * b + GB - 1))
                    for c in range(HC):
                        for t in range(2):
                            o = (c * 2 + t) * P
                            ins = nc.tensor.transpose(g[:, o:o + P], c_tok[:, 2 * n + t, c * P:(c + 1) * P], ident_sb[:])
                elif kind == "wo":
                    after_turn(pe, (f"ct{n}", b))
                    if b == 0 and n == 0:
                        pe.wait_ge(ld_late, 16 * 4)
                    for t in range(2):
                        for c in range(HC):
                            ins = nc.tensor.matmul(g[:, t * H:(t + 1) * H], ct_sb[:, c, (2 * n + t) * P:(2 * n + t + 1) * P],
                                                   wo_sb[:, c, :], start=(c == 0), stop=(c == HC - 1))
                elif kind == "xt":
                    pe.wait_ge(normed, b + 1)
                    for c in range(HC):
                        for t in range(2):
                            o = (c * 2 + t) * P
                            ins = nc.tensor.transpose(g[:, o:o + P], x_sb[:, b * TILES + 2 * n + t, c * P:(c + 1) * P],
                                                      ident_sb[:])
                elif kind == "cwt":
                    pe.wait_ge(cw_ready, 1 if b in ROUNDS[0] else 2)
                    for t in range(TILES):
                        ins = nc.tensor.transpose(g[0:E, t * P:(t + 1) * P], rt[:, 0, b * TILES + t, :], ident_sb[:])
                elif kind == "logits":
                    after_turn(pe, ("xt1", b))
                    for t in range(TILES):
                        for c in range(HC):
                            ins = nc.tensor.matmul(g[:, t * E:(t + 1) * E], xt32[:, c, t * P:(t + 1) * P], gw_sb[:, c, :],
                                                   start=(c == 0), stop=(c == HC - 1))
                ins.then_inc(ready, 1)

            def feature_chunk(n):
                b, f = FEATURES[n]
                R = frows(f)
                if n == 0:
                    pe.wait_ge(w_low, 2 * WPIECES)
                if f == NFR:
                    pe.wait_ge(x_low, 2 * b + 2)
                if n >= 2:
                    pe.wait_ge(silu_done, n - 1)
                for dst, w, s in ((ps_gate[n % 2], wg_sb, gate_ready), (ps_up[n % 2], wu_sb, up_ready)):
                    if s is up_ready and n >= 2:
                        pe.wait_ge(up_taken, n - 1)
                    for c in range(HC):
                        for p, (jw, jx) in enumerate(PASSES):
                            ins = nc.tensor.matmul(dst[0:R, :], w[:, jw, c, f * P:f * P + R], xpair[b][:, jx, c, :],
                                                   start=(c == 0 and p == 0), stop=(c == HC - 1 and p == 2))
                    ins.then_inc(s, 1)

            def value_product(m):
                G, t = m // TILES, m % TILES
                b = G // GB
                pe.wait_ge(exp_done, HG * (m + 1))
                if t == 0:
                    if G % GB == 0:
                        after_turn(pe, ("v1", b))
                    if G >= 1:
                        pe.wait_ge(o_taken, G)
                for h in range(HG):
                    ins = nc.tensor.matmul(ps_o[32 * h:32 * h + 32, :], v_sb[:, b % 2, t, (G % GB) * HG + h, :],
                                           probs[:, (HG * m + h) % 8, :], start=(t == 0), stop=(t == TILES - 1))
                ins.then_inc(pv_done, 1)

            for i, u in slots():
                t, h = u // HG, u % HG
                if 0 <= i < NG:
                    if u == 0:
                        after_stack(pe, i)
                    n = UNITS * i + u
                    if n == 0:
                        for w in range(2):
                            pe.wait_ge(rotated[w], HC)
                    used = last_use(max_bank, n, max_bank(n))
                    if used:
                        pe.wait_ge(max_taken, used)
                    nc.tensor.matmul(banks[max_bank(n)][:, :], qk[0:KS, 0, i % RING, h, t * P:(t + 1) * P],
                                     qk[0:KS, 1, i % RING, h, :], start=True, stop=True).then_inc(max_ready, 1)
                n = UNITS * i + u - LAG
                j = n // UNITS
                t, h = n % UNITS // HG, n % HG
                if 0 <= j < NG:
                    if n % UNITS == 0:
                        pe.wait_ge(maxed[j % 2], 48 * (j // 2 + 1))
                        if j == 0:
                            pe.wait_ge(ones_ready, 1)
                    bank = score_bank(n)
                    used = last_use(score_bank, n, bank)
                    if used:
                        pe.wait_ge(exp_done, used)
                    if n < SCORE_RING:
                        pe.wait_ge(max_taken, last_use(max_bank, LAG, bank))
                    if 0 <= n - (NG * UNITS - LAG) < MAX_RING:
                        pe.wait_ge(max_taken, last_use(max_bank, NG * UNITS, bank))
                    nc.tensor.matmul(banks[bank][:, :], qk[0:KS + 3, 1, j % RING, h, t * P:(t + 1) * P],
                                     qk[0:KS + 3, 0, j % RING, h, :], start=True, stop=True).then_inc(score_ready, 1)
                m = (n - VALUE_LAG) // HG
                if (n - VALUE_LAG) % HG == 0 and 0 <= m < NG * TILES:
                    value_product(m)
                for s in stages(i, u):
                    if s[0] in ROPED and s[1] == 0:
                        first_product(s[0])
                    elif banked_stage(s):
                        banked(s)
                    if s[0] == "expert":
                        feature_chunk(s[1])

            def down(b):
                if b == 0:
                    pe.wait_ge(w_low, 3 * WPIECES)
                for t in range(TILES):
                    if b == B - 1:
                        dst = banks[(6, 7, 4, 5)[t]][:, 0:H]
                        if t < 2:
                            pe.wait_ge(y_taken, TILES * b - 2 + 2 * t)
                        if t == 3:
                            pe.wait_ge(o_taken, NG)
                    else:
                        dst = ps_y[t // 2][:, (t % 2) * H:(t % 2 + 1) * H]
                        if t == 0:
                            if b == 0:
                                after_turn(pe, TURNS[-1])
                            else:
                                pe.wait_ge(y_taken, TILES * b)
                    for n in range(NF * b, NF * (b + 1)):
                        f = FEATURES[n][1]
                        if t == 0:
                            pe.wait_ge(hid_low, n + 1)
                        R = frows(f)
                        for p, (jh, jw) in enumerate(PASSES):
                            ins = nc.tensor.matmul(dst, hid[0:R, n % HRING, jh, t * P:(t + 1) * P], wd_sb[0:R, jw, f, :],
                                                   start=(n == NF * b and p == 0), stop=(n == NF * (b + 1) - 1 and p == 2))
                    ins.then_inc(y_ready, 1)

            for n in range(EARLY, len(FEATURES)):
                feature_chunk(n)
                if n >= NF and n % NF == 1:
                    down(n // NF - 1)
            down(B - 1)

        @block.scalar
        def _(act):
            def banked(s):
                name, b = s
                g = ps_gen[TURN[s] % 2]
                kind, n = name.rstrip("0123"), int(name[-1])
                act.wait_ge(ready, TURN[s] + 1)
                if kind in ("q", "k"):
                    w = int(kind == "k")
                    if n == 0:
                        act.wait_ge(resid_ready[w], HC * b)
                        act.wait_ge(elu_parts, HC * (2 * b + w - 1))
                    dst, src = rot[w][:, n, :], g[:, :]
                if kind == "v":
                    if b == 0 and n == 0:
                        act.wait_ge(init_p, 1)
                    if b >= 2:
                        act.wait_ge(pv_done, GB * TILES * (b - 1))
                    dst, src = v_sb[:, b % 2, 2 * n:2 * n + 2, :, 0:D], g[:, :].rearrange("p (t h d) -> p t h d", t=2, h=HEADS)
                if kind == "kt":
                    dst, src = kf_tok[:, 2 * n:2 * n + 2, :], g[:, :].rearrange("p (t f) -> p t f", t=2)
                if kind == "ct":
                    dst, src = ct_sb[:, :, 2 * n * P:(2 * n + 2) * P], g[:, :].rearrange("p (c t) -> p c t", c=HC)
                paired = b >= PAIRED and kind in ("q", "k", "v")
                nc.scalar.activation(dst, src, ACT.Copy, scale=1.0 / WSCALE if paired else 1.0).then_inc(taken_a, 1)

            def feature_chunk(n):
                R = frows(FEATURES[n][1])
                act.wait_ge(gate_ready, n + 1)
                if n >= 2:
                    act.wait_ge(up_taken, n - 1)
                elif n == 0:
                    act.wait_ge(pv_done, NG * TILES)
                nc.scalar.activation(gact[n % 2][0:R, :], ps_gate[n % 2][0:R, :], ACT.Silu, scale=1.0 / WSCALE)\
                    .then_inc(silu_done, 1)
                if n >= 1:
                    high_part(n - 1)

            def high_part(n):
                b, f = FEATURES[n]
                R = frows(f)
                if n == 0:
                    act.wait_ge(score_ready, NG * UNITS)
                if f >= NFR:
                    act.wait_ge(up_taken, n + 1)
                else:
                    act.wait_ge(hid_ready, routed_index(n) + 1)
                if n >= HRING:
                    act.wait_ge(y_ready, TILES * ((n - HRING) // NF + 1))
                nc.scalar.activation(hid[0:R, n % HRING, 0, :], hfull[n % 2][0:R, :], ACT.Copy).then_inc(hid_high, 1)

            for i, u in slots():
                n = UNITS * i + u - LAG
                if 0 <= n < NG * UNITS:
                    act.wait_ge(score_ready, n + 1)
                    if n >= 8:
                        act.wait_ge(pv_done, n // HG - 1)
                    nc.scalar.activation(probs[:, n % 8, :], banks[score_bank(n)][:, :], ACT.Exp, scale=SCALE)\
                        .then_inc(exp_done, 1)
                for s in to_read(i, u, LATE_FOR_SCALAR):
                    name, b = s
                    if banked_stage(s) and to_scalar(s):
                        banked(s)
                    if name == "mem0" and b == 0:
                        act.wait_ge(ld_small, 32)
                        nc.scalar.activation(gmix[:, 1, :], gmix[:, 0, :], ACT.Exp, scale=-1.0).then_inc(sigm, 1)
                    if name == "o_out":
                        act.wait_ge(pv_done, TILES * (b + 1))
                        if b >= 2:
                            act.wait_ge(ready, TURN[("ot", b - 2)] + 1)
                        nc.scalar.activation(o_sb[:, b % 2, :], ps_o[:, :], ACT.Copy).then_inc(o_taken, 1)
                    if name == "ln_sqrt":
                        after_turn(act, ("wo1", b))
                        act.wait_ge(init_v, 1)
                        nc.scalar.activation(std[:, 0, :], mv[:, :, 1], ACT.Sqrt, bias=eps_sb[:, 0:1])\
                            .then_inc(std_ready, 1)
                    if name in ("xs_high.0", "xs_high.1"):
                        n = int(name[-1])
                        act.wait_ge(ld_x[b], 16)
                        act.wait_ge(ready, TURN[("v1", b - 1)] + 1)
                        if b > PAIRED:
                            act.wait_ge(xs_low, b - PAIRED)
                        nc.scalar.activation(xpair[b - 1][:, 0, n, :], xT_sb[:, b, n, :], ACT.Copy).then_inc(xs_high, 1)
                    if name == "pw_high":
                        w = b
                        act.wait_ge((ld_q, ld_k, ld_v)[w], 16)
                        if w > 0:
                            act.wait_ge(ready, TURN[(("q1", "k1")[w - 1], PAIRED - 1)] + 1)
                            act.wait_ge(pw_low, w)
                        nc.scalar.activation(wproj[w][:, 0, :, :], w32[w].rearrange("p (c n) -> p c n", c=HC), ACT.Copy,
                                             scale=WSCALE).then_inc(pw_high, 1)
                    if name in ("x_high0", "x_high1"):
                        n = int(name[-1])
                        after_turn(act, (f"xt{n}", b))
                        if PAIRED <= b + 1 < B:
                            act.wait_ge(ready, TURN[("v1", b + 1)] + 1)
                        tokens = slice(2 * n * P, 2 * (n + 1) * P)
                        nc.scalar.activation(xpair[b][:, 0, :, tokens], xt32[:, :, tokens], ACT.Copy).then_inc(x_high, 1)
                    if name == "w_high" and b[0] != 1:
                        w, p = b
                        if p == 0:
                            act.wait_ge(ld_w[w], 16 if w < 2 else 32)
                        if w == 0 and p == 0:
                            for G in range(NG - GB, NG):
                                after_stack(act, G)
                        if w == 2 and p == 0:
                            act.wait_ge(pv_done, NG * TILES)
                        for rows, cols in w_blocks(w)[p]:
                            ins = nc.scalar.activation(wpair[w][0:rows, 0, cols], w_raw[0:rows, cols], ACT.Copy, scale=WSCALE)
                        ins.then_inc(w_high, 1)
                    if name == "expert_exp":
                        act.wait_ge(centred, b + 1)
                        n0, n1 = ROUNDS[b][0] * TILES, (ROUNDS[b][-1] + 1) * TILES
                        nc.scalar.activation(rt[:, 1, n0:n1, :], rt[:, 0, n0:n1, :], ACT.Exp).then_inc(exped, 1)
                    if name == "expert":
                        feature_chunk(b)
                    kind, _, of = name.partition("_")
                    if kind in ("split1", "split2", "exp", "relu"):
                        w, cs, done = split_step(of, b)
                        k = 2 * b + w
                        if kind == "split1":
                            act.wait_ge(rotated[w], done)
                            if b > 0:
                                for c in range(HC):
                                    after_stack(act, GB * (b - 1) + 2 * c)
                            nc.scalar.activation(part[w][0][:, cs, :], rot[w][:, cs, :], ACT.Copy).then_inc(split1[w], cs.stop - cs.start)
                        if kind == "split2":
                            act.wait_ge(resid_ready[w], done)
                            nc.scalar.activation(part[w][1][:, cs, :], resid[:, cs, :], ACT.Copy).then_inc(split2[w], cs.stop - cs.start)
                        if kind == "exp":
                            act.wait_ge(rotated[w], HC * (b + 1))
                            if k > 0:
                                act.wait_ge(feat_ready, k)
                            nc.scalar.activation(exp_r[:, cs, :], rot[w][:, cs, :], ACT.Exp)
                        if kind == "relu":
                            if b > 0:
                                act.wait_ge(ready, TURN[("kt1" if w else "mem3", b - 1)] + 1)
                            nc.scalar.activation(feat[w][:, cs, :], rot[w][:, cs, :], ACT.Relu).then_inc(elu_parts, cs.stop - cs.start)

            for n in range(EARLY, len(FEATURES)):
                feature_chunk(n)
                if n >= NF and n % NF == 6:
                    act.wait_ge(stats_ready, n // NF)
                    nc.scalar.activation(std[:, 0, :], mv[:, :, 1], ACT.Sqrt, bias=eps_sb[:, 0:1]).then_inc(std_ready, 1)
            high_part(len(FEATURES) - 1)
            for t in range(TILES):
                act.wait_ge(stats_ready, B + t)
                nc.scalar.activation(std[:, 0, t:t + 1], mv[:, t, 1:2], ACT.Sqrt, bias=eps_sb[:, 0:1]).then_inc(std_ready, 1)

        @block.gpsimd
        def _(pool):
            nc.gpsimd.memset(v_sb[:], 1.0).then_inc(init_p, 1)
            pool.wait_ge(init_p, 1)
            ones2 = float(np.frombuffer(np.array([0x3F80, 0x3F80], np.uint16).tobytes(), np.float32)[0])
            ones_rows = stack[KS:KS + 3, RING * HG * S:].bitcast(F32)
            nc.gpsimd.memset(ones_rows, ones2).then_inc(ones_ready, 1)
            pool.wait_ge(ones_ready, 1)
            chain = [0]

            def link(ins):
                chain[0] += 1
                ins.then_inc(pch, 1)
                pool.wait_ge(pch, chain[0])

            def rest(n):
                R = frows(FEATURES[n][1])
                pool.wait_ge(hid_high, n + 1)
                nc.gpsimd.tensor_tensor(hid[0:R, n % HRING, 1, :], hfull[n % 2][0:R, :], hid[0:R, n % HRING, 0, :],
                                        ALU.subtract).then_inc(hid_low, 1)

            for i, u in slots():
                for name, b in stages(i, u):
                    if name == "expert" and b > 0:
                        rest(b - 1)
                    kind, _, of = name.partition("_")
                    if kind == "rotate" and b > 0:
                        w = int(of == "k")
                        after_turn(pool, ("k1" if w else "q1", b))
                        pool.wait_ge(rotated[1 - w], HC * (b + w))
                        for n in range(2):
                            ins = nc.gpsimd.tensor_tensor(prod[:, 2 * n:2 * n + 2, :], rot[w],
                                                          cs_sb[:, n, :].unsqueeze(1).broadcast_to([P, HC, S]), ALU.mult)
                        ins.then_inc(rope_ready, 1)
                        rotate(pool, nc.gpsimd, b, int(of == "k"))
                    if kind == "resid" and (b > 0 or of[-1] == "1"):
                        first_rest(pool, nc.gpsimd, of, b)
                    if kind == "split3" and (b > 0 or of[-1] == "1"):
                        third_part(pool, nc.gpsimd, of, b)
                    if name == "maxt":
                        G = b
                        after_turn(pool, ("maxt", G))
                        if G >= 2:
                            pool.wait_ge(maxed[G % 2], 48 * (G // 2))
                        m, pt = mneg[:, G % 2, :], [x[:, G % 2, :] for x in mpart]
                        link(nc.gpsimd.tensor_copy(pt[0], m))
                        link(nc.gpsimd.tensor_tensor(mres[:], m, pt[0], ALU.subtract))
                        link(nc.gpsimd.tensor_copy(pt[1], mres[:]))
                        nc.gpsimd.tensor_tensor(pt[2], mres[:], pt[1], ALU.subtract).then_inc(mneg_split, 1)
                    if name == "xs_low":
                        pool.wait_ge(xs_high, HC * (b - PAIRED + 1))
                        nc.gpsimd.tensor_tensor(xpair[b - 1][:, 1, :, :], xT_sb[:, b, :, :], xpair[b - 1][:, 0, :, :],
                                                ALU.subtract).then_inc(xs_low, 1)
                    if name in ("x_high0", "x_high1"):
                        n = int(name[-1])
                        pool.wait_ge(x_high, 2 * b + n + 1)
                        tokens = slice(2 * n * P, 2 * (n + 1) * P)
                        nc.gpsimd.tensor_tensor(xpair[b][:, 1, :, tokens], xt32[:, :, tokens], xpair[b][:, 0, :, tokens], ALU.subtract)\
                            .then_inc(x_low, 1)

            for n in range(EARLY - 1, len(FEATURES)):
                rest(n)

        @block.vector
        def _(dve):
            chain = [0]

            def link(ins):
                chain[0] += 1
                ins.then_inc(vch, 1)
                dve.wait_ge(vch, chain[0])

            link(nc.vector.memset(eps_sb[:], EPS))
            nc.vector.memset(std[:], 1.0).then_inc(init_v, 1)

            def first_rope(kind, of):
                w, c = int(of[0] == "k"), int(of[-1])
                if kind == "sum":
                    dve.wait_ge(vch, chain[0])
                    a, b, op = ((0, 3, ALU.subtract), (1, 2, ALU.add))[c]
                    nc.vector.tensor_tensor(rot[w][:, c, :], prod[:, a, :], prod[:, b, :], op).then_inc(rotated[w], 1)
                    return
                n = int(kind == "sin")
                dve.wait_ge(ld_cs[n], 16)
                dve.wait_ge(first_ready, 2 * w + c + 1)
                if w == 1:
                    dve.wait_ge(rotated[0], (c ^ n) + 1)
                chain[0] += 1
                nc.vector.tensor_tensor(prod[:, 2 * n + c, :], banks[2 * w + c][:, :], cs_sb[:, n, :], ALU.mult).then_inc(vch, 1)

            def banked(s):
                name, b = s
                g = ps_gen[TURN[s] % 2]
                kind, n = name.rstrip("0123"), int(name[-1]) if name[-1].isdigit() else 0
                dve.wait_ge(ready, TURN[s] + 1)
                if kind == "memory":
                    for c in range(HC):
                        ins = nc.vector.tensor_tensor(mem_bd[:, b % 2, c, :].rearrange("p (h d) -> p h d", h=8),
                                                      g[:, c * 136:c * 136 + 136].rearrange("p (h d) -> p h d", h=8),
                                                      mask_sb[:], ALU.mult)
                elif kind == "mem":
                    gv = g[:, 0:HC * 136].rearrange("p (c h d) -> p c h d", c=HC, h=8)
                    link(nc.vector.reciprocal(rden[:, 0, :, :], gv[:, :, :, D]))
                    link(nc.vector.tensor_tensor(rden[:, 1, :, :], rden[:, 0, :, :],
                                                 gmix[:, 2, :].rearrange("p (c h) -> p c h", c=HC), ALU.mult))
                    for c in range(HC):
                        ins = nc.vector.tensor_tensor(
                            mem_tok[:, b % 2, n, c * P:(c + 1) * P].rearrange("p (h d) -> p h d", h=8),
                            gv[:, c, :, 0:D], rden[:, 1, c, :].unsqueeze(2).broadcast_to([P, 8, D]), ALU.mult)
                elif kind == "maxt":
                    if b >= 2:
                        dve.wait_ge(mneg_split, b - 1)
                    ins = nc.vector.tensor_scalar(mneg[:, b % 2, :], g[0:UNITS, 0:P], -1.0, None, ALU.mult)
                elif kind == "ot":
                    G, bb = b, b // GB
                    gv = g[:, :].rearrange("p (t h d) -> p t h d", t=TILES, h=HG)
                    h0 = (G % GB) * HG
                    link(nc.vector.reciprocal(rsum[:, 0, :, :], gv[:, :, :, D]))
                    link(nc.vector.tensor_tensor(rsum[:, 1, :, :], rsum[:, 0, :, :],
                                                 gmix[:, 3, h0:h0 + HG].unsqueeze(1).broadcast_to([P, TILES, HG]), ALU.mult))
                    if G % GB == 0 and bb > 0:
                        dve.wait_ge(ready, TURN[("ct1", bb - 1)] + 1)
                    for t in range(TILES):
                        ins = nc.vector.tensor_tensor(
                            c_tok[:, t, h0 * D:(h0 + HG) * D].rearrange("p (h d) -> p h d", h=HG),
                            gv[:, t, :, 0:D], rsum[:, 1, t, :].unsqueeze(2).broadcast_to([P, HG, D]), ALU.mult)
                    link(ins)
                    cv = c_tok[:, :, h0 * D:(h0 + HG) * D]
                    ins = nc.vector.tensor_tensor(cv, cv, mem_tok[:, bb % 2, :, h0 * D:(h0 + HG) * D], ALU.add)
                elif kind == "wo":
                    n0 = b * TILES + 2 * n
                    link(nc.vector.tensor_tensor(x_sb[:, n0:n0 + 2, :], g[:, :].rearrange("p (t h) -> p t h", t=2),
                                                 x_sb[:, n0:n0 + 2, :], ALU.add))
                    for t in range(2):
                        ins = nc.vector.bn_stats(stats[:, 2 * n + t, :], x_sb[:, n0 + t, :])
                    link(ins)
                    for t in range(2):
                        ins = nc.vector.bn_aggr(mv[:, 2 * n + t, :], stats[:, 2 * n + t, :])
                elif kind == "xt":
                    if b > 0 and n == 0:
                        dve.wait_ge(x_low, 2 * b)
                        dve.wait_ge(ready, TURN[("logits", b - 1)] + 1)
                    ins = nc.vector.tensor_copy(xt32[:, :, 2 * n * P:(2 * n + 2) * P],
                                                g[:, :].rearrange("p (c t) -> p c t", c=HC))
                elif kind == "cwt":
                    if b >= 2:
                        dve.wait_ge(cw_stored[b % 2], 16 * (b // 2))
                    ins = nc.vector.tensor_scalar(cwT[:, b % 2, :], g[0:E, :], 1.0 / WSCALE, None, ALU.mult)
                elif kind == "logits":
                    ins = nc.vector.tensor_copy(lg_sb[:, b * TILES:(b + 1) * TILES, :],
                                                g[:, 0:TILES * E].rearrange("p (t e) -> p t e", e=E))
                ins.then_inc(taken_v, 1)

            def normalise(b, k):
                dve.wait_ge(std_ready, k + 1)
                link(nc.vector.reciprocal(std[:, 1, :], std[:, 0, :]))
                for t in range(TILES):
                    row = x_sb[:, b * TILES + t, :]
                    ins = nc.vector.tensor_scalar(row, row, mv[:, t, 0:1], std[:, 1, t:t + 1], ALU.subtract, ALU.mult)
                ins.then_inc(normed, 1)

            def feature_chunk(n):
                b, f = FEATURES[n]
                R = frows(f)
                dve.wait_ge(silu_done, n + 1)
                dve.wait_ge(up_ready, n + 1)
                if n >= 2:
                    dve.wait_ge(hid_low, n - 1)
                full = hfull[n % 2][0:R, :]
                if f >= NFR:
                    nc.vector.scalar_tensor_tensor(out=full, in0=ps_up[n % 2][0:R, :], scalar=1.0 / WSCALE,
                                                   in1=gact[n % 2][0:R, :], op0=ALU.mult, op1=ALU.mult).then_inc(up_taken, 1)
                    return
                m = routed_index(n)
                nc.vector.tensor_tensor(hmid[n % 2][:, :], ps_up[n % 2][:, :], gact[n % 2][:, :], ALU.mult).then_inc(up_taken, 1)
                dve.wait_ge(up_taken, n + 1)
                dve.wait_ge(cw_loaded[m % CW_RING], 16 * cw_loads(m))
                nc.vector.tensor_tensor(full, cw_rows[m % CW_RING], hmid[n % 2][:, :], ALU.mult).then_inc(hid_ready, 1)

            def across(a):
                return a.unsqueeze(2).broadcast_to([P, a.shape[1], E])

            def tiles_of(r):
                return slice(ROUNDS[r][0] * TILES, (ROUNDS[r][-1] + 1) * TILES)

            def centre(r):
                N = tiles_of(r)
                dve.wait_ge(taken_v, nth(("logits", ROUNDS[r][-1])))
                link(nc.vector.tensor_reduce(rs[:, 0, N], lg_sb[:, N, :], AX_X, ALU.max))
                nc.vector.tensor_tensor(rt[:, 0, N, :], lg_sb[:, N, :], across(rs[:, 0, N]), ALU.subtract).then_inc(centred, 1)

            def weigh(r):
                N = tiles_of(r)
                dve.wait_ge(exped, r + 1)
                p = rt[:, 1, N, :]
                link(nc.vector.tensor_reduce(rs[:, 1, N], p, AX_X, ALU.add))
                link(nc.vector.reciprocal(rs[:, 2, N], rs[:, 1, N]))
                link(nc.vector.tensor_tensor(p, p, across(rs[:, 2, N]), ALU.mult))
                ranks = rank_sb[:].unsqueeze(1).broadcast_to([P, N.stop - N.start, E])
                for w in range(2):
                    top, hit = rs[:, 3 + w, N], rt[:, 2 + w, N, :]
                    link(nc.vector.tensor_reduce(top, p, AX_X, ALU.max))
                    link(nc.vector.tensor_tensor(hit, p, across(top), ALU.is_equal))
                    link(nc.vector.tensor_tensor(hit, hit, ranks, ALU.mult))
                    link(nc.vector.tensor_reduce(rs[:, 5, N], hit, AX_X, ALU.max))
                    link(nc.vector.tensor_tensor(hit, hit, across(rs[:, 5, N]), ALU.is_equal))
                    if w == 0:
                        link(nc.vector.scalar_tensor_tensor(out=p, in0=hit, scalar=-4.0, in1=p, op0=ALU.mult, op1=ALU.add))
                    link(nc.vector.tensor_tensor(hit, hit, across(top), ALU.mult))
                link(nc.vector.tensor_tensor(rs[:, 6, N], rs[:, 3, N], rs[:, 4, N], ALU.add))
                link(nc.vector.tensor_scalar(rs[:, 6, N], rs[:, 6, N], 1e-20, None, ALU.add))
                link(nc.vector.reciprocal(rs[:, 7, N], rs[:, 6, N]))
                cw = rt[:, 0, N, :]
                link(nc.vector.tensor_tensor(cw, rt[:, 2, N, :], rt[:, 3, N, :], ALU.add))
                nc.vector.tensor_tensor(cw, cw, across(rs[:, 7, N]), ALU.mult).then_inc(cw_ready, 1)

            for i, u in slots():
                if 0 <= i < NG:
                    n = UNITS * i + u
                    t, h = u // HG, u % HG
                    dve.wait_ge(max_ready, n + 1)
                    if u == 0 and i >= 2:
                        dve.wait_ge(ready, TURN[("maxt", i - 2)] + 1)
                    nc.vector.tensor_reduce(mx[:, i % 2, h * TILES + t:h * TILES + t + 1], banks[max_bank(n)][:, :], AX_X, ALU.max)\
                        .then_inc(max_taken, 1)
                for s in to_read(i, u, LATE_FOR_VECTOR):
                    name, b = s
                    if banked_stage(s) and not to_scalar(s):
                        if s == ("memory", 0):
                            dve.wait_ge(ld_small, 32)
                        if s == ("wo0", 0):
                            dve.wait_ge(ld_late, 16 * 4)
                        if s == ("mem0", 0):
                            dve.wait_ge(sigm, 1)
                            link(nc.vector.tensor_scalar(gmix[:, 2, :], gmix[:, 1, :], 1.0, None, ALU.add))
                            link(nc.vector.reciprocal(gmix[:, 2, :], gmix[:, 2, :]))
                            link(nc.vector.tensor_scalar(gmix[:, 3, :], gmix[:, 2, :], -1.0, 1.0, ALU.mult, ALU.add))
                        banked(s)
                    kind, _, of = name.partition("_")
                    if kind == "feat":
                        feature(dve, nc.vector, b, int(of == "k"))
                    if kind in ("cos", "sin", "sum"):
                        first_rope(kind, of)
                    if kind == "resid" and b == 0 and of[-1] == "0":
                        first_rest(dve, nc.vector, of, b)
                    if kind == "split3" and b == 0 and of[-1] == "0":
                        third_part(dve, nc.vector, of, b)
                    if name == "ln_apply":
                        normalise(b, b)
                    if name == "pw_low":
                        w = b
                        dve.wait_ge(pw_high, w + 1)
                        nc.vector.scalar_tensor_tensor(out=wproj[w][:, 1, :, :], in0=w32[w].rearrange("p (c n) -> p c n", c=HC),
                                                       scalar=WSCALE, in1=wproj[w][:, 0, :, :],
                                                       op0=ALU.mult, op1=ALU.subtract).then_inc(pw_low, 1)
                    if name == "w_high" and b[0] == 1:
                        w, p = b
                        if p == 0:
                            dve.wait_ge(ld_w[w], 16)
                            for G in range(NG - GB, NG):
                                after_stack(dve, G)
                        for rows, cols in w_blocks(w)[p]:
                            ins = nc.vector.tensor_scalar(wpair[w][0:rows, 0, cols], w_raw[0:rows, cols], WSCALE, None, ALU.mult)
                        ins.then_inc(w_high, 1)
                    if name == "w_low":
                        w, p = b
                        dve.wait_ge(w_high, WPIECES * w + p + 1)
                        for rows, cols in w_blocks(w)[p]:
                            ins = nc.vector.scalar_tensor_tensor(
                                out=wpair[w][0:rows, 1, cols], in0=w_raw[0:rows, cols], scalar=WSCALE,
                                in1=wpair[w][0:rows, 0, cols], op0=ALU.mult, op1=ALU.subtract)
                        ins.then_inc(w_low, 1)
                    if name == "centre":
                        centre(b)
                    if name == "weigh":
                        weigh(b)
                    if name == "expert":
                        feature_chunk(b)

            def finish_tile(b, t):
                n = b * TILES + t
                dve.wait_ge(y_ready, n + 1)
                y = banks[(6, 7, 4, 5)[t]][:, 0:H] if b == B - 1 else ps_y[t // 2][:, (t % 2) * H:(t % 2 + 1) * H]
                nc.vector.scalar_tensor_tensor(out=x_sb[:, n, :], in0=y, scalar=1.0 / WSCALE, in1=x_sb[:, n, :],
                                               op0=ALU.mult, op1=ALU.add).then_inc(y_taken, 1)
                dve.wait_ge(y_taken, n + 1)
                link(nc.vector.bn_stats(stats[:, t, :], x_sb[:, n, :]))
                ins = nc.vector.bn_aggr(mv[:, t, :], stats[:, t, :])
                if t == TILES - 1 or b == B - 1:
                    ins.then_inc(stats_ready, 1)

            for n in range(EARLY, len(FEATURES)):
                b, k = n // NF, n % NF
                if b > 0 and k == 2:
                    for t in range(TILES):
                        if t % 2 == 0:
                            dve.wait_ge(y_ready, (b - 1) * TILES + t + 2)
                        finish_tile(b - 1, t)
                feature_chunk(n)
                if b > 0 and k == 7:
                    normalise(b - 1, B + b - 1)
            for t in range(TILES):
                finish_tile(B - 1, t)
                dve.wait_ge(std_ready, 2 * B + t)
                link(nc.vector.reciprocal(std[:, 1, t:t + 1], std[:, 0, t:t + 1]))
                row = x_sb[:, (B - 1) * TILES + t, :]
                nc.vector.tensor_scalar(row, row, mv[:, t, 0:1], std[:, 1, t:t + 1], ALU.subtract, ALU.mult).then_inc(normed, 1)


def kernel(**inputs):
    import concourse.bacc as bacc
    from concourse.bass_utils import run_bass_kernel_spmd

    def arr(name):
        return np.asarray(inputs["L0_" + name])

    order = np.array([(c * 8 + h) * D + d
                      for c in range(HC) for d in range(D) for h in range(8)])
    row_head = (order[:P] // D)
    inv_freq = (np.float32(1.0) / np.float32(10000.0) ** (np.arange(0, H, 2, dtype=np.float32) / np.float32(H))).astype(np.float32)
    angle = (np.arange(S, dtype=np.float32)[None, :] * inv_freq[order[:P]][:, None]).astype(np.float32)
    blockmask = np.repeat((row_head[:, None] == np.arange(8)[None, :]).astype(np.float32), D + 1, axis=1)
    xs = arr("attn_hidden_states").reshape(B * S, H)

    def stackT(routed, shared):
        return np.concatenate([routed.reshape(E * F, H), shared], axis=0)

    arrays = {
        "x": xs, "xT": xs.T,
        "wqT": arr("attn_Wq")[order].T, "wkT": arr("attn_Wk")[order].T,
        "wvT": arr("attn_Wv").T, "woT": arr("attn_Wo").T,
        "gate": arr("attn_gate").reshape(1, HEADS),
        "cos": np.cos(angle), "sin": np.sin(angle), "blockmask": blockmask,
        "ident": np.eye(P, dtype=np.float32),
        "gwT": arr("ffn_gate_weight").T,
        "rank": np.tile(np.arange(E, 0, -1, dtype=np.float32), (P, 1)),
        "wgT": stackT(arr("ffn_w_gate"), arr("ffn_sw_gate")).T,
        "wuT": stackT(arr("ffn_w_up"), arr("ffn_sw_up")).T,
        "wdT": np.concatenate([arr("ffn_w_down").transpose(0, 2, 1).reshape(E * F, H), arr("ffn_sw_down").T], axis=0),
    }
    nc = bacc.Bacc("TRN2", target_bir_lowering=False, num_devices=1)
    aps = {}
    for name in list(arrays):
        a = np.ascontiguousarray(arrays[name])
        arrays[name] = a
        aps[name] = nc.dram_tensor(name, a.shape, mybir.dt.from_np(a.dtype), kind="ExternalInput").ap()
    out = nc.dram_tensor("out", (B * S, H), F32, kind="ExternalOutput").ap()
    cw_dram = nc.dram_tensor("cw_dram", (E, B * S), F32, kind="Internal").ap()
    build_block(nc, out=out, cw_dram=cw_dram, **aps)
    r = run_bass_kernel_spmd(nc, [arrays], core_ids=[0])
    return r.results[0]["out"].reshape(B, S, H)
```
